# Optimizing a Trainium2 kernel written in Bass

```python
import numpy as np
import jax
import jax.numpy as jnp

def _softmax(x, axis=-1):
    return jax.nn.softmax(x, axis=axis)

def _gelu(x):
    return jax.nn.gelu(x, approximate=True)

def _silu(x):
    return jax.nn.silu(x)

def _sigmoid(x):
    return jax.nn.sigmoid(x)

def _layernorm(x, axis=-1, eps=1e-05):
    m = jnp.mean(x, axis=axis, keepdims=True)
    v = jnp.var(x, axis=axis, keepdims=True)
    return (x - m) / jnp.sqrt(v + eps)

def _scatter_add(tgt, idx, src, axis=0):
    return tgt.at[idx].add(src)

def _segment_sum(src, seg, n):
    return jax.ops.segment_sum(src, seg, n)
kernel_name = 'mk_vit_tower_d1_tok_img512_r4_77302f'

def setup_inputs(seed: int=0):
    np.random.seed(seed)
    _w = jnp.asarray

    def _rec_inputs():
        import jax
        import jax.numpy as jnp
        _rk = jax.random.key(seed)
        x = -0.000147625 + 0.999875 * jax.random.normal(jax.random.fold_in(_rk, 1), (128, 3, 224, 224), jnp.float32)
        return x
    x = _rec_inputs()

    def _L0_tok_setup():
        import jax, jax.numpy as jnp
        import numpy as np
        N_PATCHES = 8
        PATCH = 28
        C = 3
        IN_D = C * PATCH * PATCH
        HID = 128
        SEQ = N_PATCHES * N_PATCHES + 1

        def _positional_embedding(seq_len, dim):
            i = np.arange(seq_len)[:, None].astype(np.float32)
            j = np.arange(dim)[None, :].astype(np.float32)
            ang = i / np.power(100000.0, j / dim)
            pe = np.where(j % 2 == 0, np.sin(ang), np.cos(ang))
            return jnp.asarray(pe, dtype=jnp.float32)
        key = jax.random.key(seed)
        k1, k2, k3, k4 = jax.random.split(key, 4)
        B = 64
        X = jax.random.normal(k1, (B, C, 224, 224), dtype=jnp.float32)
        bound = 1.0 / np.sqrt(IN_D)
        W = jax.random.uniform(k2, (HID, IN_D), minval=-bound, maxval=bound, dtype=jnp.float32)
        b = jax.random.uniform(k3, (HID,), minval=-bound, maxval=bound, dtype=jnp.float32)
        class_token = jax.random.uniform(k4, (1, HID), dtype=jnp.float32)
        pos_embed = _positional_embedding(SEQ, HID)
        return {'X': X, 'W': W, 'b': b, 'class_token': class_token, 'pos_embed': pos_embed}
    _L0_tok_all = _L0_tok_setup()
    _L0_tok_in = {k: v for k, v in _L0_tok_all.items() if k in ('W', 'b', 'class_token', 'pos_embed')}
    del _L0_tok_all

    def _L0_attn_setup():
        import jax, jax.numpy as jnp
        import numpy as np
        NUM_HEADS = 16
        EPS = 1e-15
        key = jax.random.key(seed)
        k1, k2, k3, k4 = jax.random.split(key, 4)
        B, N, C = (4, 4096, 128)
        x = jax.random.normal(k1, (B, N, C), dtype=jnp.float32)
        qkv_weight = jax.random.normal(k2, (3 * C, C), dtype=jnp.float32) * 0.02
        proj_weight = jax.random.normal(k3, (C, C), dtype=jnp.float32) * 0.02
        proj_bias = jax.random.normal(k4, (C,), dtype=jnp.float32) * 0.02
        return {'x': x, 'qkv_weight': qkv_weight, 'proj_weight': proj_weight, 'proj_bias': proj_bias}
    _L0_attn_all = _L0_attn_setup()
    _L0_attn_in = {k: v for k, v in _L0_attn_all.items() if k in ('qkv_weight', 'proj_weight', 'proj_bias')}
    del _L0_attn_all

    def _L0_ffn_setup():
        import jax, jax.numpy as jnp
        import numpy as np
        B, T, D = (4, 2048, 128)
        E, F, CAP = (8, 512, 1024)
        key = jax.random.key(seed)
        ks = jax.random.split(key, 6)
        s = 0.02
        return {'x': jax.random.normal(ks[0], (B, T, D), dtype=jnp.float32), 'Wr': jax.random.normal(ks[1], (D, E), dtype=jnp.float32) * s, 'W1': jax.random.normal(ks[2], (E, D, F), dtype=jnp.float32) * s, 'b1': jax.random.normal(ks[3], (E, F), dtype=jnp.float32) * s, 'W2': jax.random.normal(ks[4], (E, F, D), dtype=jnp.float32) * s, 'b2': jax.random.normal(ks[5], (E, D), dtype=jnp.float32) * s}
    _L0_ffn_all = _L0_ffn_setup()
    _L0_ffn_in = {k: v for k, v in _L0_ffn_all.items() if k in ('Wr', 'W1', 'b1', 'W2', 'b2')}
    del _L0_ffn_all
    return {'x': x, 'L0_tok_W': _L0_tok_in['W'], 'L0_tok_b': _L0_tok_in['b'], 'L0_tok_class_token': _L0_tok_in['class_token'], 'L0_tok_pos_embed': _L0_tok_in['pos_embed'], 'L0_attn_qkv_weight': _L0_attn_in['qkv_weight'], 'L0_attn_proj_weight': _L0_attn_in['proj_weight'], 'L0_attn_proj_bias': _L0_attn_in['proj_bias'], 'L0_ffn_Wr': _L0_ffn_in['Wr'], 'L0_ffn_W1': _L0_ffn_in['W1'], 'L0_ffn_b1': _L0_ffn_in['b1'], 'L0_ffn_W2': _L0_ffn_in['W2'], 'L0_ffn_b2': _L0_ffn_in['b2']}

def reference(x, L0_tok_W, L0_tok_b, L0_tok_class_token, L0_tok_pos_embed, L0_attn_qkv_weight, L0_attn_proj_weight, L0_attn_proj_bias, L0_ffn_Wr, L0_ffn_W1, L0_ffn_b1, L0_ffn_W2, L0_ffn_b2):
    import jax
    import jax.numpy as jnp

    def _L0_tok_ref(X, W, b, class_token, pos_embed):
        import jax, jax.numpy as jnp
        import numpy as np
        N_PATCHES = 8
        PATCH = 28
        C = 3
        IN_D = C * PATCH * PATCH
        HID = 128
        SEQ = N_PATCHES * N_PATCHES + 1

        def _positional_embedding(seq_len, dim):
            i = np.arange(seq_len)[:, None].astype(np.float32)
            j = np.arange(dim)[None, :].astype(np.float32)
            ang = i / np.power(100000.0, j / dim)
            pe = np.where(j % 2 == 0, np.sin(ang), np.cos(ang))
            return jnp.asarray(pe, dtype=jnp.float32)
        B = X.shape[0]
        patches = X.reshape(B, C, N_PATCHES, PATCH, N_PATCHES, PATCH)
        patches = patches.transpose(0, 2, 4, 1, 3, 5).reshape(B, N_PATCHES * N_PATCHES, IN_D)
        tokens = jnp.einsum('bpi,hi->bph', patches, W) + b
        cls = jnp.broadcast_to(class_token[None, :, :], (B, 1, HID))
        tokens = jnp.concatenate([cls, tokens], axis=1)
        return tokens * pos_embed[None, :, :]

    def _L0_attn_ref(x, qkv_weight, proj_weight, proj_bias):
        import jax, jax.numpy as jnp
        import numpy as np
        NUM_HEADS = 16
        EPS = 1e-15
        B, N, C = x.shape
        H = NUM_HEADS
        D = C // H
        qkv = (x @ qkv_weight.T).reshape(B, N, 3, C)
        q = jax.nn.relu(qkv[:, :, 0]).reshape(B, N, H, D)
        k = jax.nn.relu(qkv[:, :, 1]).reshape(B, N, H, D)
        v = qkv[:, :, 2].reshape(B, N, H, D)
        qf = q.astype(jnp.float32)
        kf = k.astype(jnp.float32)
        vf = v.astype(jnp.float32)
        v_pad = jnp.concatenate([vf, jnp.ones_like(vf[..., :1])], axis=-1)
        vk = jnp.einsum('bnhc,bnhd->bhcd', v_pad, kf)
        vk_q = jnp.einsum('bnhd,bhcd->bnhc', qf, vk)
        proj_input = (vk_q[..., :-1] / (vk_q[..., -1:] + EPS)).astype(x.dtype).reshape(B, N, C)
        return proj_input @ proj_weight.T + proj_bias

    def _L0_ffn_ref(x, Wr, W1, b1, W2, b2):
        import jax, jax.numpy as jnp
        import numpy as np
        B, T, D = (4, 2048, 128)
        E, F, CAP = (8, 512, 1024)
        Bb, Tt, Dd = x.shape
        N = Bb * Tt
        C = min(CAP, N)
        x_flat = x.reshape(N, Dd)
        logits = x_flat @ Wr
        probs = jax.nn.softmax(logits, axis=0)
        vals, idx = jax.lax.top_k(probs.T, C)
        selected = x_flat[idx]
        h = jax.nn.gelu(jnp.einsum('ecd,edf->ecf', selected, W1) + b1[:, None, :], approximate=False)
        out_e = jnp.einsum('ecf,efd->ecd', h, W2) + b2[:, None, :]
        weighted = vals[..., None] * out_e
        output = jnp.zeros_like(x_flat).at[idx.reshape(-1)].add(weighted.reshape(-1, Dd))
        return output.reshape(Bb, Tt, Dd)
    h = _L0_tok_ref(x, L0_tok_W, L0_tok_b, L0_tok_class_token, L0_tok_pos_embed)
    h = h + _L0_attn_ref(_layernorm(h, axis=-1), L0_attn_qkv_weight, L0_attn_proj_weight, L0_attn_proj_bias)
    h = h + _L0_ffn_ref(_layernorm(h, axis=-1), L0_ffn_Wr, L0_ffn_W1, L0_ffn_b1, L0_ffn_W2, L0_ffn_b2)
    return h

_drawn_inputs = setup_inputs


def setup_inputs(seed=0):
    import zlib

    import numpy as np

    out = dict(_drawn_inputs(seed))
    spreads = {}
    factors = {'L0_ffn_Wr': 25.188,
     'L0_ffn_W1': 31.936,
     'L0_ffn_b1': 64.0,
     'L0_ffn_W2': 27.848,
     'L0_ffn_b2': 196.067,
     'L0_tok_class_token': 2.763}
    for name, (base, spread) in spreads.items():
        noise = np.random.default_rng([zlib.crc32(name.encode()), seed]).standard_normal(out[name].shape)
        drawn = base * np.exp(spread * noise) if base else spread * noise
        out[name] = jnp.asarray(drawn.astype(out[name].dtype))
    for name, factor in factors.items():
        out[name] = (out[name] * factor).astype(out[name].dtype)
    return out
```

```python
from contextlib import ExitStack

import numpy as np

import concourse.bass as bass
from concourse import mybir

F32 = mybir.dt.float32
F16 = mybir.dt.float16
BF16 = mybir.dt.bfloat16
I32 = mybir.dt.int32
ALU = mybir.AluOpType
ACT = mybir.ActivationFunctionType
AX = mybir.AxisListType

IMAGES, CHANNELS, SIDE, PATCH = 128, 3, 224, 28
GRID = SIDE // PATCH
PATCHES = GRID * GRID
SEQ = PATCHES + 1
HID = 128
IN_D = CHANNELS * PATCH * PATCH
HEAD_D = 8
EXPERTS, FFN, CAP = 8, 512, 1024
TOKENS = IMAGES * SEQ

GROUP = 8
GROUPS = IMAGES // GROUP
GP = GROUP * PATCHES
GT = GROUP * SEQ
HALF_I = GROUP // 2
HT = HALF_I * SEQ
CHUNKS = IN_D // 128
TAIL = IN_D - CHUNKS * 128
SLOTS = [(0, 5), (5, 10), (10, 15), (15, CHUNKS)]
TILE = 104
TPG = GT // TILE
TILES = TOKENS // TILE
SEGS = 16
KPS = TILES // SEGS
SEG = TOKENS // SEGS
ROW = HID + EXPERTS
LO, HI = 64, 16
RT = CAP // 128
FT = FFN // 128
LN_EPS, DEN_EPS = 1e-5, 1e-15

C_CENTRE, C_MEAN, C_HEAD, C_SAME, C_BEFORE, C_ONE, C_IDENT = (128 * n for n in range(7))
C_PCOL = C_IDENT + 128
C_BITS = C_PCOL + 1
C_TILE = C_BITS + 31
C_COLS = C_TILE + EXPERTS * TILES


def constants():
    c = np.zeros((128, C_COLS), np.float32)
    i = np.arange(128)
    c[:, C_CENTRE:C_CENTRE + 128] = np.eye(128) - 1 / 128
    c[:, C_MEAN:C_MEAN + 128] = 1 / 128
    c[:, C_HEAD:C_HEAD + 128] = i[:, None] // HEAD_D == i[None] // HEAD_D
    c[:, C_ONE:C_ONE + 128] = 1
    same = i[:, None] % EXPERTS == i[None] % EXPERTS
    c[:, C_SAME:C_SAME + 128] = same
    c[:, C_BEFORE:C_BEFORE + 128] = same & (i[:, None] // EXPERTS < i[None] // EXPERTS)
    c[:, C_IDENT:C_IDENT + 128] = np.eye(128)
    c[:, C_PCOL] = i
    c[:, C_BITS:C_BITS + 31] = 2.0 ** np.arange(30, -1, -1)
    c[:, C_TILE:] = np.tile(np.arange(TILES), EXPERTS)
    return c


def tower(nc, xmain, xtail, wmain, wtail, cst, tokb, cls, posT, wqkvT, projT, projb, wr, w1, b1, w2, b2, out):
    rows_dram = nc.dram_tensor("rows_dram", (TOKENS, ROW), F32).ap()
    ctx = ExitStack()
    with ctx:
        def sb(stack, name, shape, dt=F32):
            return stack.enter_context(nc.sbuf_tensor(name, shape, dt))

        def sem(name):
            return ctx.enter_context(nc.semaphore(name))

        C = sb(ctx, "C", [128, C_COLS])
        Wr = sb(ctx, "Wr", [128, EXPERTS])
        logits = sb(ctx, "logits", [TILE, KPS, SEGS, EXPERTS])
        idx = sb(ctx, "idx", [128, EXPERTS, RT], I32)
        centre, mean, heads = (C[:, o:o + 128] for o in (C_CENTRE, C_MEAN, C_HEAD))
        same, before, ones, ident = (C[:, o:o + 128] for o in (C_SAME, C_BEFORE, C_ONE, C_IDENT))
        ident_wr = sb(ctx, "ident_wr", [128, ROW])
        eps_ln = sb(ctx, "eps_ln", [128, 1])
        eps_den = sb(ctx, "eps_den", [128, 1])

        A = ExitStack()
        X = sb(A, "X", [128, CHUNKS + 1, GP])
        W = sb(A, "W", [128, CHUNKS + 1, HID])
        Tokb = sb(A, "Tokb", [128, 1])
        Cls = sb(A, "Cls", [128, 1])
        Pos = sb(A, "Pos", [128, SEQ])
        Wqkv = sb(A, "Wqkv", [128, 3 * HID])
        Proj = sb(A, "Proj", [128, HID])
        Projb = sb(A, "Projb", [128, 1])
        c_col = sb(A, "c_col", [128, 6])
        c_row = sb(A, "c_row", [1, 2 * HID + 1])
        kv_cls = sb(A, "kv_cls", [128, HID + 1])
        h = sb(A, "h", [128, GROUP, SEQ])
        h2 = sb(A, "h2", [128, GT])
        xn2 = sb(A, "xn2", [128, GT])
        rows = sb(A, "rows", [TILE, TPG, HID])
        orow = sb(A, "orow", [TILE, TPG, HID])
        two = range(2)
        sq = [sb(A, f"sq{i}", [128, HT]) for i in two]
        std = [sb(A, f"std{i}", [128, HT]) for i in two]
        rstd = [sb(A, f"rstd{i}", [128, HT]) for i in two]
        xn = [sb(A, f"xn{i}", [128, HALF_I, SEQ]) for i in two]
        xp = [sb(A, f"xp{i}", [128, HALF_I, PATCHES]) for i in two]
        q = [sb(A, f"q{i}", [128, HALF_I, SEQ]) for i in two]
        qk = [sb(A, f"qk{i}", [128, HALF_I, SEQ]) for i in two]
        ksum = [sb(A, f"ksum{i}", [128, HALF_I]) for i in two]
        kk = [sb(A, f"kk{i}", [128, 2, HID]) for i in two]
        vv = [sb(A, f"vv{i}", [128, 2, HID + 1]) for i in two]
        kvm = [sb(A, f"kvm{i}", [128, HALF_I, HID]) for i in two]
        kvf = [sb(A, f"kvf{i}", [128, HALF_I, HID]) for i in two]
        den = [sb(A, f"den{i}", [128, HT]) for i in two]
        rden = [sb(A, f"rden{i}", [128, HT]) for i in two]
        att = [sb(A, f"att{i}", [128, HT]) for i in two]
        A.close()

        B = ExitStack()
        lt = sb(B, "lt", [128, SEG])
        junk = sb(B, "junk", [128, SEG], BF16)
        ge = sb(B, "ge", [128, SEG])
        eq = sb(B, "eq", [128, SEG])
        scan = sb(B, "scan", [128, SEG])
        slot = sb(B, "slot", [128, SEG])
        rmax = sb(B, "rmax", [128, 1])
        mrow = sb(B, "mrow", [1, EXPERTS])
        mb = sb(B, "mb", [TILE, EXPERTS])
        pex = sb(B, "pex", [TILE, KPS * SEGS, EXPERTS])
        psum_e = sb(B, "psum_e", [TILE, EXPERTS])
        prs = sb(B, "prs", [TILE, EXPERTS])
        prob = sb(B, "prob", [TILE, TILES, EXPERTS])
        cnt = sb(B, "cnt", [128, 1], F16)
        zero = sb(B, "zero", [128, 1])
        cand = sb(B, "cand", [128, 1], I32)
        flip = sb(B, "flip", [128, 1], I32)
        bits = sb(B, "bits", [128, 32], I32)
        same16 = sb(B, "same16", [128, 128], F16)
        tot = sb(B, "tot", [128, 4])
        room = sb(B, "room", [128, 1])
        sloti = sb(B, "sloti", [TILE, EXPERTS, TILES], I32)
        part_i = sb(B, "part_i", [TILE, 2, EXPERTS * TILES], I32)
        part = sb(B, "part", [TILE, 2, EXPERTS * TILES], BF16)
        tile_b = sb(B, "tile_b", [TILE, EXPERTS * TILES], BF16)
        oh_lo = sb(B, "oh_lo", [TILE, EXPERTS, LO, TILES], BF16)
        oh_hi = sb(B, "oh_hi", [TILE, 2, HI, EXPERTS, TILES], BF16)
        val = sb(B, "val", [128, EXPERTS // 2, 2, 2, HI])
        tok = sb(B, "tok", [128, EXPERTS // 2, 2, HI], I32)
        B.close()

        D = ExitStack()
        W1 = [sb(D, f"W1{i}", [128, FFN]) for i in two]
        B1 = [sb(D, f"B1{i}", [128, FT]) for i in two]
        W2 = [sb(D, f"W2{i}", [128, FT, HID]) for i in two]
        B2 = [sb(D, f"B2{i}", [128, HID]) for i in two]
        take = [sb(D, f"take{i}", [128, RT], I32) for i in two]
        got = [sb(D, f"got{i}", [128, RT, ROW]) for i in two]
        xe = [sb(D, f"xe{i}", [128, CAP]) for i in two]
        hid = [sb(D, f"hid{i}", [128, FT, CAP]) for i in two]
        yb = [sb(D, f"yb{i}", [128, RT, HID]) for i in two]
        yv = [sb(D, f"yv{i}", [128, RT, HID]) for i in two]
        D.close()

        bank = [ctx.enter_context(nc.psum_tensor(f"bank{i}", [128, 512], F32)) for i in range(8)]
        emb = bank[0]
        t0, t1, t2 = (bank[1], bank[2]), (bank[3], bank[4]), (bank[5], bank[6])
        spare = bank[7]

        s_const, s_w = sem("const_loaded"), sem("embed_weights_loaded")
        s_x = [sem(f"x_loaded{i}") for i in range(len(SLOTS))]
        s_xt = sem("xtail_loaded")
        s_x_used = [sem(f"x_used{i}") for i in range(len(SLOTS) - 1)]
        s_emb, s_h = sem("embedded"), sem("h_ready")
        s_set, s_ones, s_hc = sem("setup_done"), sem("ones_ready"), sem("h_cls_ready")
        s_cp, s_ca, s_cv = sem("cls_pe"), sem("cls_act"), sem("cls_dve")
        s_c1, s_sq1, s_v1, s_std1, s_r1, s_xn = (sem(n) for n in ("centred1", "sq1", "var1", "std1", "rstd1", "xn_ready"))
        s_xp = sem("xn_patches_ready")
        s_q, s_kv, s_qs, s_kvs = (sem(n) for n in ("q_psum", "kv_psum", "q_ready", "kv_ready"))
        s_kvp, s_kvm, s_ks, s_kvf, s_qk = (sem(n) for n in ("kvprod_psum", "kv_masked", "ksum_ready", "kv_full", "qk_ready"))
        s_num, s_den, s_dens, s_rden, s_att = (sem(n) for n in ("num_psum", "den_psum", "den_ready", "rden_ready", "att_ready"))
        s_pr, s_h2 = sem("proj_psum"), sem("h2_ready")
        s_c2, s_sq2, s_v2, s_std2, s_r2, s_xn2 = (sem(n) for n in ("centred2", "sq2", "var2", "std2", "rstd2", "xn2_ready"))
        s_row, s_tr, s_rows, s_orow = sem("rows_psum"), sem("otr_psum"), sem("rows_ready"), sem("orow_ready")
        s_rst, s_ost = sem("rows_stored"), sem("out_stored")
        s_ltp, s_lt, s_rmax, s_rmaxt, s_mrow, s_mbp, s_mb, s_pex, s_exp, s_psum, s_tote, s_prs, s_probr = (
            sem(n) for n in ("lt_psum", "lt_ready", "rowmax", "rowmax_t", "mrow", "max_psum", "max_ready", "pex", "exp_ready",
                             "partial_sum", "sum_psum", "rsum", "prob_ready"))
        s_bset, s_cnt, s_tot, s_rej, s_cand = (sem(n) for n in ("search_setup", "counted", "totalled", "rejected", "candidate"))
        s_sel, s_gtot, s_room, s_chosen, s_selt, s_slot, s_slotp = (
            sem(n) for n in ("ties_scanned", "gt_totals", "room", "chosen", "slots_before", "slot_ready", "slot_psum"))
        s_part, s_ohl, s_ohp, s_ohu, s_listp, s_list, s_idx = (
            sem(n) for n in ("slot_parts", "onehot_lo", "onehot_hi_p", "onehot_hi_u", "list_psum", "list_ready", "idx_ready"))
        s_prob = sem("probs_stored")
        s_take = sem("take_ready")
        s_wc = [sem(f"expert_loaded{i}") for i in two]
        s_got = [sem(f"gathered{i}") for i in two]
        s_xep, s_xe, s_up, s_hid = sem("xe_psum"), sem("xe_ready"), sem("up_psum"), sem("hid_ready")
        s_dn, s_yb, s_yv, s_add = sem("down_psum"), sem("yb_ready"), sem("yv_ready"), sem("added")

        block = ctx.enter_context(nc.Block())

        def first(g):
            return isinstance(g, int) and g == 0

        @block.sync
        def _(sp):
            for dst, src in ((C[:], cst), (Wr[:], wr), (Tokb[:], tokb), (Cls[:], cls), (Pos[:], posT),
                             (Wqkv[:], wqkvT), (Proj[:], projT), (Projb[:], projb)):
                sp.dma_start(dst, src).then_inc(s_const, 16)

            def load(g, s):
                lo, hi = SLOTS[s]
                sp.dma_start(X[:, lo:hi, :], xmain[bass.ds(g, 1), :, lo:hi, :].rearrange("a p c n -> p (a c) n"))\
                    .then_inc(s_x[s], 16)
                if s == len(SLOTS) - 1:
                    sp.dma_start(X[:TAIL, CHUNKS, :], xtail[bass.ds(g, 1), :, :].rearrange("a p n -> p (a n)"))\
                        .then_inc(s_xt, 16)

            def reload(g):
                for s in range(len(SLOTS)):
                    if s < len(SLOTS) - 1:
                        sp.wait_ge(s_x_used[s], g)
                    else:
                        sp.wait_ge(s_emb, g)
                    load(g, s)

            def store(a):
                sp.wait_ge(s_rows, 2 * a + 2)
                sp.dma_start(rows_dram.rearrange("(g k p) c -> g p k c", p=TILE, k=TPG)[bass.ds(a, 1), :, :, :HID]
                             .rearrange("g p k c -> (g p) k c"), rows[:]).then_inc(s_rst, 16)
                sp.wait_ge(s_orow, 2 * a + 2)
                sp.dma_start(out.rearrange("(g k p) c -> g p k c", p=TILE, k=TPG)[bass.ds(a, 1), :, :, :]
                             .rearrange("g p k c -> (g p) k c"), orow[:]).then_inc(s_ost, 16)

            for s, (lo, hi) in enumerate(SLOTS):
                sp.dma_start(W[:, lo:hi, :], wmain[:, lo:hi, :]).then_inc(s_w, 16)
                if s == 0:
                    sp.dma_start(W[:TAIL, CHUNKS, :], wtail).then_inc(s_w, 16)
                load(0, s)
            reload(1)
            with sp.Fori(2, GROUPS) as g:
                reload(g)
                store(g - 2)
            store(GROUPS - 2)
            store(GROUPS - 1)

            sp.wait_ge(s_probr, 1)
            sp.wait_ge(s_rst, 16 * GROUPS)
            sp.dma_start(rows_dram.rearrange("(u p) c -> p u c", p=TILE)[:, :, HID:ROW], prob[:]).then_inc(s_prob, 16)

            def weights(e, i):
                sp.dma_start(W1[i][:], w1[bass.ds(e, 1), :, :].rearrange("a p n -> p (a n)")).then_inc(s_wc[i], 16)
                sp.dma_start(B1[i][:], b1[bass.ds(e, 1), :, :].rearrange("a p n -> p (a n)")).then_inc(s_wc[i], 16)
                sp.dma_start(W2[i][:], w2[bass.ds(e, 1), :, :, :].rearrange("a p f n -> p (a f) n")).then_inc(s_wc[i], 16)
                sp.dma_start(B2[i][:], b2[bass.ds(e, 1), :].broadcast_to([128, HID])).then_inc(s_wc[i], 16)

            sp.wait_ge(s_prob, 16)
            sp.wait_ge(s_listp, 1)
            sp.wait_ge(s_idx, 1)
            weights(0, 0)
            weights(1, 1)
            with sp.Fori(1, EXPERTS // 2) as j:
                for i in two:
                    sp.wait_ge(s_yv, 4 * j + 2 * i - 2)
                    weights(j * 2 + i, i)

        @block.tensor
        def _(pe):
            def embed(g, lo, hi):
                for c in range(lo, hi):
                    for s, (a, b) in enumerate(SLOTS):
                        if c == a:
                            pe.wait_ge(s_x[s], 16 * g + 16)
                    if c == 0 and not first(g):
                        pe.wait_ge(s_h, g)
                    if c == CHUNKS:
                        pe.wait_ge(s_xt, 16 * g + 16)
                    k = TAIL if c == CHUNKS else 128
                    last = nc.tensor.matmul(emb[:], W[:k, c, :], X[:k, c, :], start=(c == 0), stop=(c == CHUNKS))
                    for s, (a, b) in enumerate(SLOTS[:-1]):
                        if c == b - 1:
                            last.then_inc(s_x_used[s], 1)
                    if c == CHUNKS:
                        last.then_inc(s_emb, 1)

            def centre1(a, i):
                pe.wait_ge(s_h, a + 1)
                if not first(a):
                    pe.wait_ge(s_orow, 2 * a)
                nc.tensor.matmul(t0[i][:, :HT], centre, h[:, HALF_I * i:HALF_I * (i + 1), :],
                                 start=True, stop=True).then_inc(s_c1, 1)

            def var1(a, i):
                pe.wait_ge(s_sq1, 2 * a + i + 1)
                nc.tensor.matmul(t1[i][:, :HT], mean, sq[i][:], start=True, stop=True).then_inc(s_v1, 1)

            def qkv(a, i):
                pe.wait_ge(s_xn, 2 * a + i + 1)
                nc.tensor.matmul(t1[i][:, :HT], Wqkv[:, :HID], xn[i][:], start=True, stop=True).then_inc(s_q, 1)
                pe.wait_ge(s_xp, 2 * a + i + 1)
                for pair in two:
                    last = nc.tensor.matmul(t0[i][:, 256 * pair:256 * (pair + 1)], xp[i][:, 2 * pair:2 * pair + 2, :].rearrange("p a b -> p (a b)"),
                                            Wqkv[:, HID:], start=True, stop=True)
                last.then_inc(s_kv, 1)

            def kvprod(a, i):
                pe.wait_ge(s_kvs, 2 * a + i + 1)
                pe.wait_ge(s_qs, 2 * a + i + 1)
                if not first(a):
                    pe.wait_ge(s_rows, 2 * a)
                for im in range(HALF_I):
                    r = slice(64 * (im % 2), 64 * (im % 2) + 64)
                    dst = (t2, t1)[im % 2][i]
                    last = nc.tensor.matmul(dst[:, 129 * (im // 2):129 * (im // 2) + 129], kk[i][r, im // 2, :],
                                            vv[i][r, im // 2, :], start=True, stop=True)
                last.then_inc(s_kvp, 1)

            def attend(a, i):
                pe.wait_ge(s_kvf, 2 * a + i + 1)
                for im in range(HALF_I):
                    last = nc.tensor.matmul(t0[i][:, SEQ * im:SEQ * (im + 1)], kvf[i][:, im, :], q[i][:, im, :],
                                            start=True, stop=True)
                last.then_inc(s_num, 1)
                pe.wait_ge(s_qk, 2 * a + i + 1)
                nc.tensor.matmul(t1[i][:, :HT], heads, qk[i][:], start=True, stop=True).then_inc(s_den, 1)

            def project(a, i):
                pe.wait_ge(s_att, 2 * a + i + 1)
                nc.tensor.matmul(t2[i][:, :HT], Proj[:], att[i][:], start=True, stop=True).then_inc(s_pr, 1)

            def centre2(a, i):
                pe.wait_ge(s_h2, 2 * a + i + 1)
                nc.tensor.matmul(t0[i][:, :HT], centre, h2[:, HT * i:HT * (i + 1)], start=True, stop=True).then_inc(s_c2, 1)

            def var2(a, i):
                pe.wait_ge(s_sq2, 2 * a + i + 1)
                nc.tensor.matmul(t1[i][:, :HT], mean, sq[i][:], start=True, stop=True).then_inc(s_v2, 1)

            def to_rows(a):
                pe.wait_ge(s_xn2, 2 * a + 2)
                for k in range(TPG):
                    last = nc.tensor.matmul(t2[k // 3][:TILE, ROW * (k % 3):ROW * (k % 3 + 1)],
                                            xn2[:, TILE * k:TILE * (k + 1)], ident_wr[:], start=True, stop=True)
                    if k in (2, TPG - 1):
                        last.then_inc(s_row, 1)
                for k in range(TPG):
                    last = nc.tensor.transpose(t0[k // 4][:TILE, HID * (k % 4):HID * (k % 4 + 1)],
                                               h2[:, TILE * k:TILE * (k + 1)], ident)
                    if k in (3, TPG - 1):
                        last.then_inc(s_tr, 1)

            pe.wait_ge(s_set, 1)
            nc.tensor.matmul(t0[0][:, 0:1], centre, c_col[:, 0:1], start=True, stop=True).then_inc(s_cp, 1)
            pe.wait_ge(s_ca, 1)
            nc.tensor.matmul(t1[0][:, 0:1], mean, c_col[:, 1:2], start=True, stop=True).then_inc(s_cp, 1)
            pe.wait_ge(s_cv, 2)
            nc.tensor.matmul(t0[0][0:1, 0:256], c_col[:, 4:5], Wqkv[:, HID:], start=True, stop=True).then_inc(s_cp, 1)
            pe.wait_ge(s_ca, 4)
            nc.tensor.matmul(t1[0][:, 0:HID + 1], c_row[:, 0:HID], c_row[:, HID:], start=True, stop=True).then_inc(s_cp, 1)

            pe.wait_ge(s_w, 16 * (len(SLOTS) + 1))
            embed(0, 0, CHUNKS + 1)
            with pe.Fori(1, GROUPS) as g:
                a = g - 1
                embed(g, 0, 2)
                centre1(a, 0), centre1(a, 1)
                embed(g, 2, 4)
                var1(a, 0), var1(a, 1)
                embed(g, 4, 7)
                qkv(a, 0), qkv(a, 1)
                embed(g, 7, 9)
                kvprod(a, 0), kvprod(a, 1)
                embed(g, 9, 12)
                attend(a, 0), attend(a, 1)
                embed(g, 12, 14)
                project(a, 0), project(a, 1)
                embed(g, 14, 15)
                centre2(a, 0), centre2(a, 1)
                embed(g, 15, 17)
                var2(a, 0), var2(a, 1)
                embed(g, 17, CHUNKS + 1)
                to_rows(a)
            for step in (centre1, var1, qkv, kvprod, attend, project, centre2, var2):
                step(GROUPS - 1, 0), step(GROUPS - 1, 1)
            to_rows(GROUPS - 1)

            pe.wait_ge(s_rows, 2 * GROUPS)
            pe.wait_ge(s_orow, 2 * GROUPS)
            for k in range(KPS):
                last = nc.tensor.transpose(bank[k // 4][:, TILE * (k % 4):TILE * (k % 4 + 1)], logits[:, k, :, :].rearrange("p s e -> p (s e)"), ident[:TILE, :TILE])
            last.then_inc(s_ltp, 1)
            pe.wait_ge(s_rmax, 1)
            nc.tensor.transpose(bank[2][:1, :128], rmax[:], ident).then_inc(s_rmaxt, 1)
            pe.wait_ge(s_mrow, 1)
            nc.tensor.matmul(bank[3][:TILE, :EXPERTS], ones[:1, :TILE], mrow[:], start=True, stop=True).then_inc(s_mbp, 1)

            def total(n):
                pe.wait_ge(s_cnt, n + 1)
                nc.tensor.matmul(bank[5 + n % 2][:, 0:1], same16[:], cnt[:], start=True, stop=True).then_inc(s_tot, 1)

            for n in range(2):
                total(n)
            pe.wait_ge(s_psum, 1)
            nc.tensor.matmul(bank[4][:TILE, :EXPERTS], ones[:TILE, :TILE], psum_e[:], start=True, stop=True).then_inc(s_tote, 1)
            for n in range(2, 32):
                total(n)
            pe.wait_ge(s_sel, 1)
            nc.tensor.matmul(bank[5][:, 0:1], same, tot[:, 0:1], start=True, stop=True)
            nc.tensor.matmul(bank[5][:, 1:2], before, tot[:, 1:2], start=True, stop=True).then_inc(s_gtot, 1)
            pe.wait_ge(s_chosen, 1)
            nc.tensor.matmul(bank[6][:, 0:1], before, scan[:, SEG - 1:SEG], start=True, stop=True).then_inc(s_selt, 1)
            pe.wait_ge(s_slot, 1)
            for k in range(KPS):
                last = nc.tensor.transpose(bank[k // 4][:TILE, 128 * (k % 4):128 * (k % 4 + 1)],
                                           slot[:, TILE * k:TILE * (k + 1)], ident)
            last.then_inc(s_slotp, 1)
            pe.wait_ge(s_ohl, LO)
            pe.wait_ge(s_ohp, HI)
            pe.wait_ge(s_ohu, HI)
            for pair in range(EXPERTS // 2):
                for u in range(TILES):
                    last = nc.tensor.matmul(bank[7][:, 64 * pair:64 * (pair + 1)],
                                            oh_lo[:, 2 * pair:2 * pair + 2, :, u].rearrange("p e a -> p (e a)"),
                                            oh_hi[:, :, :, 2 * pair:2 * pair + 2, u].rearrange("p v a e -> p v e a"),
                                            start=(pair == 0 and u == 0), stop=(u == TILES - 1), skip_group_check=True)
            last.then_inc(s_listp, 1)

            def run_expert(j, i):
                n = 2 * j + i
                start = first(j) and i == 0
                pe.wait_ge(s_got[i], 16 * RT * (j + 1))
                if not start:
                    pe.wait_ge(s_xe, 2 * n)
                for r in range(RT):
                    last = nc.tensor.transpose(bank[r // 4][:, 128 * (r % 4):128 * (r % 4 + 1)], got[i][:, r, :HID], ident)
                    if r % 4 == 3:
                        last.then_inc(s_xep, 1)
                pe.wait_ge(s_wc[i], 64 * (j + 1))
                for half in two:
                    pe.wait_ge(s_xe, 2 * n + half + 1)
                    for f in range(FT):
                        m = FT * half + f
                        if not start or m >= 4:
                            pe.wait_ge(s_hid, 8 * n + m - 3)
                        nc.tensor.matmul(bank[2 + m % 4][:], W1[i][:, 128 * f:128 * (f + 1)],
                                         xe[i][:, 512 * half:512 * (half + 1)], start=True, stop=True).then_inc(s_up, 1)
                for r in range(RT):
                    if r % 4 == 0:
                        pe.wait_ge(s_hid, 8 * n + r + 4)
                        if not start:
                            pe.wait_ge(s_yb, 2 * n + r // 4 - 1)
                    for f in range(FT):
                        last = nc.tensor.matmul(bank[6 + r // 4][:, 128 * (r % 4):128 * (r % 4 + 1)],
                                                hid[i][:, f, 128 * r:128 * (r + 1)], W2[i][:, f, :],
                                                start=(f == 0 and r % 4 == 0), stop=(f == FT - 1), skip_group_check=True)
                    if r % 4 == 3:
                        last.then_inc(s_dn, 1)

            run_expert(0, 0)
            run_expert(0, 1)
            with pe.Fori(1, EXPERTS // 2) as j:
                run_expert(j, 0)
                run_expert(j, 1)

        @block.scalar
        def _(act):
            def square(src, i, ready, n, done):
                act.wait_ge(ready, n)
                nc.scalar.activation(sq[i][:], src[i][:, :HT], ACT.Square).then_inc(done, 1)

            def root(src, i, ready, n, done):
                act.wait_ge(ready, n)
                nc.scalar.activation(std[i][:], src[i][:, :HT], ACT.Sqrt, bias=eps_ln[:]).then_inc(done, 1)

            def keys_values(a, i):
                act.wait_ge(s_kv, 2 * a + i + 1)
                kv = t0[i][:].rearrange("p (b c) -> p b c", b=2)
                nc.scalar.activation(kk[i][:], kv[:, :, :HID], ACT.Relu)
                nc.scalar.activation(vv[i][:, :, :HID], kv[:, :, HID:], ACT.Copy).then_inc(s_kvs, 1)

            def denominator(a, i):
                act.wait_ge(s_den, 2 * a + i + 1)
                nc.scalar.activation(den[i][:], t1[i][:, :HT], ACT.Identity, bias=eps_den[:]).then_inc(s_dens, 1)

            def to_rows(a):
                for n, (lo, hi) in enumerate(((0, 3), (3, TPG))):
                    act.wait_ge(s_row, 2 * a + n + 1)
                    if n == 0 and not first(a):
                        act.wait_ge(s_rst, 16 * a)
                    r = t2[n][:TILE, :ROW * (hi - lo)].rearrange("p (k c) -> p k c", c=ROW)
                    nc.scalar.activation(logits[:, lo:hi, bass.ds(a, 1), :].rearrange("p k s e -> p k (s e)"), r[:, :, HID:], ACT.Copy)
                    nc.scalar.activation(rows[:, lo:hi, :], r[:, :, :HID], ACT.Copy).then_inc(s_rows, 1)
                for n, (lo, hi) in enumerate(((0, 4), (4, TPG))):
                    act.wait_ge(s_tr, 2 * a + n + 1)
                    if n == 0 and not first(a):
                        act.wait_ge(s_ost, 16 * a)
                    nc.scalar.activation(orow[:, lo:hi, :], t0[n][:TILE, :HID * (hi - lo)].rearrange("p (k c) -> p k c", c=HID),
                                         ACT.Copy).then_inc(s_orow, 1)

            def group(a):
                square(t0, 0, s_c1, 2 * a + 1, s_sq1), square(t0, 1, s_c1, 2 * a + 2, s_sq1)
                root(t1, 0, s_v1, 2 * a + 1, s_std1), root(t1, 1, s_v1, 2 * a + 2, s_std1)
                keys_values(a, 0), keys_values(a, 1)
                denominator(a, 0), denominator(a, 1)
                square(t0, 0, s_c2, 2 * a + 1, s_sq2), square(t0, 1, s_c2, 2 * a + 2, s_sq2)
                root(t1, 0, s_v2, 2 * a + 1, s_std2), root(t1, 1, s_v2, 2 * a + 2, s_std2)
                to_rows(a)

            act.wait_ge(s_ones, 1)
            act.wait_ge(s_cp, 1)
            nc.scalar.activation(c_col[:, 1:2], t0[0][:, 0:1], ACT.Square).then_inc(s_ca, 1)
            act.wait_ge(s_cp, 2)
            nc.scalar.activation(c_col[:, 2:3], t1[0][:, 0:1], ACT.Sqrt, bias=eps_ln[:]).then_inc(s_ca, 1)
            act.wait_ge(s_cp, 3)
            nc.scalar.activation(c_row[:, :HID], t0[0][:1, :HID], ACT.Relu).then_inc(s_ca, 1)
            nc.scalar.activation(c_row[:, HID:2 * HID], t0[0][:1, HID:256], ACT.Copy).then_inc(s_ca, 1)

            group(0)
            with act.Fori(1, GROUPS) as a:
                group(a)

            act.wait_ge(s_pex, 1)
            nc.scalar.activation(pex[:], pex[:], ACT.Exp).then_inc(s_exp, 1)

            def hidden(j, i):
                n = 2 * j + i
                act.wait_ge(s_wc[i], 64 * (j + 1))
                for m in range(2 * FT):
                    half, f = m // FT, m % FT
                    act.wait_ge(s_up, 8 * n + m + 1)
                    if m == 0 and not first(j):
                        act.wait_ge(s_dn, 2 * n - 2)
                    nc.scalar.activation(hid[i][:, f, 512 * half:512 * (half + 1)], bank[2 + m % 4][:], ACT.Gelu,
                                         bias=B1[i][:, f:f + 1]).then_inc(s_hid, 1)

            hidden(0, 0)
            hidden(0, 1)
            with act.Fori(1, EXPERTS // 2) as j:
                hidden(j, 0)
                hidden(j, 1)

        @block.vector
        def _(dve):
            def evacuate(g):
                dve.wait_ge(s_emb, g + 1)
                nc.vector.scalar_tensor_tensor(
                    out=h[:, :, 1:], in0=emb[:].rearrange("p (b n) -> p b n", b=GROUP), scalar=Tokb[:],
                    in1=Pos[:, 1:].unsqueeze(1).broadcast_to([128, GROUP, PATCHES]), op0=ALU.add, op1=ALU.mult).then_inc(s_h, 1)

            def norm(a, i, ready, rdone, dst, done):
                n = 2 * a + i + 1
                dve.wait_ge(ready, n)
                nc.vector.reciprocal(rstd[i][:], std[i][:]).then_inc(rdone, 1)
                dve.wait_ge(rdone, n)
                nc.vector.tensor_tensor(dst, t0[i][:, :HT], rstd[i][:], ALU.mult).then_inc(done, 1)

            def norm1(a, i):
                norm(a, i, s_std1, s_r1, xn[i][:].rearrange("p a b -> p (a b)"), s_xn)
                dve.wait_ge(s_xn, 2 * a + i + 1)
                nc.vector.tensor_copy(xp[i][:], xn[i][:, :, 1:]).then_inc(s_xp, 1)

            def norm2(a, i):
                norm(a, i, s_std2, s_r2, xn2[:, HT * i:HT * (i + 1)], s_xn2)

            def queries(a, i):
                dve.wait_ge(s_q, 2 * a + i + 1)
                nc.vector.tensor_scalar(q[i][:].rearrange("p a b -> p (a b)"), t1[i][:, :HT], 0.0, None, ALU.max).then_inc(s_qs, 1)

            def mask(a, i):
                dve.wait_ge(s_kvp, 2 * a + i + 1)
                for n, t in enumerate((t2, t1)):
                    kv = t[i][:, :258].rearrange("p (b c) -> p b c", b=2)
                    last = nc.vector.tensor_tensor(kvm[i][:, n::2, :], kv[:, :, :HID],
                                                   heads.unsqueeze(1).broadcast_to([128, 2, HID]), ALU.mult)
                last.then_inc(s_kvm, 1)
                for n, t in enumerate((t2, t1)):
                    kv = t[i][:, :258].rearrange("p (b c) -> p b c", b=2)
                    last = nc.vector.tensor_scalar(ksum[i][:, n::2].unsqueeze(2), kv[:, :, HID:], kv_cls[:, HID:], None, ALU.add)
                last.then_inc(s_ks, 1)

            def attention(a, i):
                dve.wait_ge(s_dens, 2 * a + i + 1)
                nc.vector.reciprocal(rden[i][:], den[i][:]).then_inc(s_rden, 1)
                dve.wait_ge(s_rden, 2 * a + i + 1)
                dve.wait_ge(s_num, 2 * a + i + 1)
                nc.vector.tensor_tensor(att[i][:], t0[i][:, :HT], rden[i][:], ALU.mult).then_inc(s_att, 1)

            def residual(a, i):
                dve.wait_ge(s_pr, 2 * a + i + 1)
                nc.vector.scalar_tensor_tensor(
                    out=h2[:, HT * i:HT * (i + 1)], in0=t2[i][:, :HT], scalar=Projb[:],
                    in1=h[:, HALF_I * i:HALF_I * (i + 1), :].rearrange("p a b -> p (a b)"),
                    op0=ALU.add, op1=ALU.add).then_inc(s_h2, 1)

            def group(a):
                for step in (norm1, queries, mask, attention, residual, norm2):
                    step(a, 0), step(a, 1)

            nc.vector.memset(eps_ln[:], LN_EPS)
            nc.vector.memset(eps_den[:], DEN_EPS)
            nc.vector.memset(c_row[:, 2 * HID:], 1.0)
            for i in two:
                last = nc.vector.memset(vv[i][:, :, HID:], 1.0)
            last.then_inc(s_ones, 1)
            dve.wait_ge(s_const, 16 * 8)
            nc.vector.tensor_tensor(c_col[:, 0:1], Cls[:], Pos[:, 0:1], ALU.mult).then_inc(s_hc, 1)
            nc.vector.tensor_copy(ident_wr[:, :HID], ident)
            nc.vector.tensor_copy(ident_wr[:, HID:], Wr[:])
            dve.wait_ge(s_hc, 1)
            nc.vector.tensor_copy(h[:, :, 0], c_col[:, 0:1].broadcast_to([128, GROUP])).then_inc(s_set, 1)
            dve.wait_ge(s_ca, 2)
            nc.vector.reciprocal(c_col[:, 3:4], c_col[:, 2:3]).then_inc(s_cv, 1)
            dve.wait_ge(s_cv, 1)
            nc.vector.tensor_tensor(c_col[:, 4:5], t0[0][:, 0:1], c_col[:, 3:4], ALU.mult).then_inc(s_cv, 1)
            dve.wait_ge(s_cp, 4)
            nc.vector.tensor_tensor(kv_cls[:, :HID], t1[0][:, :HID], heads, ALU.mult)
            nc.vector.tensor_copy(kv_cls[:, HID:], t1[0][:, HID:HID + 1]).then_inc(s_cv, 1)
            dve.wait_ge(s_cv, 3)

            evacuate(0)
            with dve.Fori(1, GROUPS) as g:
                group(g - 1)
                evacuate(g)
            group(GROUPS - 1)

            dve.wait_ge(s_rst, 16 * GROUPS)
            dve.wait_ge(s_ost, 16 * GROUPS)
            dve.wait_ge(s_orow, 2 * GROUPS)
            nc.vector.tensor_copy(bits[:, :31], C[:, C_BITS:C_BITS + 31])
            nc.vector.memset(zero[:], 0.0)
            nc.vector.tensor_copy(same16[:], same).then_inc(s_bset, 1)
            dve.wait_ge(s_ltp, 1)
            nc.vector.tensor_copy(lt[:, :4 * TILE], bank[0][:, :4 * TILE])
            nc.vector.tensor_copy(lt[:, 4 * TILE:], bank[1][:, :TILE]).then_inc(s_lt, 1)
            dve.wait_ge(s_lt, 1)
            dve.wait_ge(s_bset, 1)
            nc.vector.reduce_max(rmax[:], lt[:], axis=AX.X).then_inc(s_rmax, 1)
            dve.wait_ge(s_rmaxt, 1)
            nc.vector.reduce_max(mrow[:], bank[2][:1, :128].rearrange("p (s e) -> p e s", e=EXPERTS), axis=AX.X).then_inc(s_mrow, 1)
            dve.wait_ge(s_mbp, 1)
            nc.vector.tensor_copy(mb[:], bank[3][:TILE, :EXPERTS]).then_inc(s_mb, 1)
            dve.wait_ge(s_mb, 1)
            nc.vector.tensor_tensor(pex[:], logits[:].rearrange("p k s e -> p (k s) e"), mb[:].unsqueeze(1).broadcast_to([TILE, TILES, EXPERTS]),
                                    ALU.subtract).then_inc(s_pex, 1)

            def count(n, threshold):
                nc.vector.tensor_scalar(junk[:], lt[:], threshold, None, ALU.is_ge, ALU.add, accum_out=cnt[:]).then_inc(s_cnt, 1)

            BIT = [1 << (30 - n) for n in range(31)]
            count(0, 0.0)
            dve.wait_ge(s_tot, 1)
            nc.vector.tensor_scalar(flip[:], bank[5][:, 0:1], float(CAP), -1.0, ALU.is_lt, ALU.mult).then_inc(s_rej, 1)
            dve.wait_ge(s_rej, 1)
            nc.vector.tensor_scalar(cand[:], flip[:], BIT[0], None, ALU.bitwise_xor).then_inc(s_cand, 1)
            for n in range(1, 32):
                dve.wait_ge(s_cand, n)
                count(n, cand[:].bitcast(F32))
                if n == 1:
                    dve.wait_ge(s_exp, 1)
                    nc.vector.reduce_sum(psum_e[:], pex[:].rearrange("p u e -> p e u"), axis=AX.X).then_inc(s_psum, 1)
                    dve.wait_ge(s_tote, 1)
                    nc.vector.reciprocal(prs[:], bank[4][:TILE, :EXPERTS]).then_inc(s_prs, 1)
                    dve.wait_ge(s_prs, 1)
                    nc.vector.tensor_tensor(prob[:].rearrange("p (s k) e -> p k s e", k=KPS),
                                            pex[:].rearrange("p (k s) e -> p k s e", k=KPS),
                                            prs[:].unsqueeze(1).unsqueeze(1).broadcast_to([TILE, KPS, SEGS, EXPERTS]), ALU.mult).then_inc(s_probr, 1)
                dve.wait_ge(s_tot, n + 1)
                nc.vector.tensor_scalar(flip[:], bank[5 + n % 2][:, 0:1], float(CAP), float(BIT[n - 1]), ALU.is_lt, ALU.mult)\
                    .then_inc(s_rej, 1)
                dve.wait_ge(s_rej, n + 1)
                if n < 31:
                    nc.vector.scalar_tensor_tensor(out=cand[:], in0=cand[:], scalar=BIT[n], in1=flip[:],
                                                   op0=ALU.bitwise_xor, op1=ALU.bitwise_xor).then_inc(s_cand, 1)
                else:
                    nc.vector.tensor_tensor(cand[:], cand[:], flip[:], ALU.bitwise_xor).then_inc(s_cand, 1)
            dve.wait_ge(s_cand, 32)

            T = cand[:].bitcast(F32)
            nc.vector.tensor_scalar(ge[:], lt[:], T, None, ALU.is_gt, ALU.add, accum_out=tot[:, 0:1])
            nc.vector.tensor_scalar(eq[:], lt[:], T, None, ALU.is_equal, ALU.add, accum_out=tot[:, 1:2]).then_inc(s_sel, 1)
            dve.wait_ge(s_sel, 1)
            nc.vector.tensor_tensor_scan(scan[:], eq[:], eq[:], 0.0, ALU.add, ALU.max).then_inc(s_sel, 1)
            dve.wait_ge(s_gtot, 1)
            nc.vector.tensor_scalar(tot[:, 2:3], bank[5][:, 0:1], -1.0, float(CAP), ALU.mult, ALU.add).then_inc(s_sel, 1)
            dve.wait_ge(s_sel, 3)
            nc.vector.tensor_tensor(room[:], tot[:, 2:3], bank[5][:, 1:2], ALU.subtract).then_inc(s_room, 1)
            dve.wait_ge(s_room, 1)
            nc.vector.scalar_tensor_tensor(out=eq[:], in0=scan[:], scalar=room[:], in1=eq[:],
                                           op0=ALU.is_le, op1=ALU.mult).then_inc(s_room, 1)
            dve.wait_ge(s_room, 2)
            nc.vector.tensor_tensor(ge[:], ge[:], eq[:], ALU.add).then_inc(s_room, 1)
            dve.wait_ge(s_room, 3)
            nc.vector.tensor_tensor_scan(scan[:], ge[:], ge[:], 0.0, ALU.add, ALU.max).then_inc(s_chosen, 1)
            dve.wait_ge(s_chosen, 1)
            dve.wait_ge(s_selt, 1)
            nc.vector.tensor_copy(room[:], bank[6][:, 0:1]).then_inc(s_room, 1)
            dve.wait_ge(s_room, 4)
            nc.vector.scalar_tensor_tensor(out=scan[:], in0=scan[:], scalar=room[:], in1=ge[:],
                                           op0=ALU.add, op1=ALU.mult).then_inc(s_room, 1)
            dve.wait_ge(s_room, 5)
            nc.vector.tensor_scalar(slot[:], scan[:], -1.0, None, ALU.add).then_inc(s_slot, 1)
            dve.wait_ge(s_slotp, 1)
            for n, (lo, hi) in enumerate(((0, 4), (4, KPS))):
                last = nc.vector.tensor_copy(sloti[:].rearrange("p e (s k) -> p k s e", k=KPS)[:, lo:hi],
                                             bank[n][:TILE, :128 * (hi - lo)].rearrange("p (k s e) -> p k s e", s=SEGS, e=EXPERTS))
            last.then_inc(s_part, 1)
            dve.wait_ge(s_part, 1)
            nc.vector.tensor_scalar(part_i[:, 0, :], sloti[:].rearrange("p e u -> p (e u)"), LO - 1, None, ALU.bitwise_and)
            nc.vector.tensor_scalar(part_i[:, 1, :], sloti[:].rearrange("p e u -> p (e u)"), LO.bit_length() - 1, None, ALU.arith_shift_right)
            nc.vector.tensor_copy(tile_b[:], C[:TILE, C_TILE:]).then_inc(s_part, 1)
            dve.wait_ge(s_part, 2)
            nc.vector.tensor_copy(part[:], part_i[:]).then_inc(s_part, 1)
            dve.wait_ge(s_part, 3)
            for v in range(LO):
                nc.vector.tensor_scalar(oh_lo[:, :, v, :],
                                        part[:, 0, :].rearrange("p (e u) -> p e u", e=EXPERTS), float(v), None, ALU.is_equal).then_inc(s_ohl, 1)
            for v in range(HI):
                nc.vector.tensor_scalar(oh_hi[:, 0, v].rearrange("p e u -> p (e u)"), part[:, 1, :], float(v), C[:TILE, C_PCOL:C_PCOL + 1],
                                        ALU.is_equal, ALU.mult).then_inc(s_ohp, 1)
            for v in range(HI):
                nc.vector.scalar_tensor_tensor(out=oh_hi[:, 1, v].rearrange("p e u -> p (e u)"), in0=part[:, 1, :], scalar=float(v), in1=tile_b[:],
                                               op0=ALU.is_equal, op1=ALU.mult).then_inc(s_ohu, 1)
            dve.wait_ge(s_listp, 1)
            nc.vector.tensor_copy(val[:].rearrange("p a v e h -> p (a v e h)"), bank[7][:, :256]).then_inc(s_list, 1)
            dve.wait_ge(s_list, 1)
            nc.vector.scalar_tensor_tensor(out=tok[:], in0=val[:, :, 1], scalar=float(TILE), in1=val[:, :, 0],
                                           op0=ALU.mult, op1=ALU.add).then_inc(s_list, 1)
            dve.wait_ge(s_list, 2)
            dve.wait_ge(s_prob, 16)
            for e2 in two:
                for h2_ in two:
                    last = nc.vector.tensor_copy(
                        idx[64 * h2_:64 * h2_ + 64].rearrange("p (a e) r -> p a e r", e=2)[:, :, e2, :],
                        tok[64 * e2:64 * e2 + 64].rearrange("p a e (r h) -> p a e r h", h=2)[:, :, e2, :, h2_])
            last.then_inc(s_idx, 1)

            def inputs(j, i):
                n = 2 * j + i
                for half in two:
                    dve.wait_ge(s_xep, 2 * n + half + 1)
                    nc.vector.tensor_copy(xe[i][:, 512 * half:512 * (half + 1)], bank[half][:]).then_inc(s_xe, 1)

            def outputs(j, i):
                n = 2 * j + i
                for half in two:
                    dve.wait_ge(s_dn, 2 * n + half + 1)
                    dve.wait_ge(s_wc[i], 64 * (j + 1))
                    r = slice(4 * half, 4 * half + 4)
                    nc.vector.tensor_tensor(yb[i][:, r, :], bank[6 + half][:].rearrange("p (r c) -> p r c", c=HID),
                                            B2[i][:].unsqueeze(1).broadcast_to([128, 4, HID]), ALU.add).then_inc(s_yb, 1)
                    dve.wait_ge(s_yb, 2 * n + half + 1)
                    if not first(j):
                        dve.wait_ge(s_add, 16 * RT * (n - 1))
                    e = HID + n
                    nc.vector.tensor_tensor(yv[i][:, r, :], yb[i][:, r, :],
                                            got[i][:, r, bass.ds(e, 1)].broadcast_to([128, 4, HID]), ALU.mult).then_inc(s_yv, 1)

            inputs(0, 0), outputs(0, 0), inputs(0, 1), outputs(0, 1)
            with dve.Fori(1, EXPERTS // 2) as j:
                inputs(j, 0), outputs(j, 0), inputs(j, 1), outputs(j, 1)

        @block.gpsimd
        def _(pool):
            def full(a, i):
                pool.wait_ge(s_kvm, 2 * a + i + 1)
                nc.gpsimd.tensor_tensor(kvf[i][:], kvm[i][:], kv_cls[:, :HID].unsqueeze(1).broadcast_to([128, HALF_I, HID]),
                                        ALU.add).then_inc(s_kvf, 1)
                pool.wait_ge(s_ks, 2 * a + i + 1)
                nc.gpsimd.tensor_tensor(qk[i][:], q[i][:], ksum[i][:].unsqueeze(2).broadcast_to([128, HALF_I, SEQ]),
                                        ALU.mult).then_inc(s_qk, 1)

            pool.wait_ge(s_cv, 3)
            with pool.Fori(0, GROUPS) as a:
                full(a, 0), full(a, 1)

            def gather(e, i):
                pool.wait_ge(s_take, e + 1)
                pool.wait_ge(s_idx, 1)
                for r in range(RT):
                    nc.gpsimd.indirect_dma_start(
                        out=got[i][:, r, :], out_offset=None, in_=rows_dram,
                        in_offset=bass.IndirectOffsetOnAxis(ap=take[i][:, r:r + 1], axis=0)).then_inc(s_got[i], 16)

            def indices(e, i):
                nc.gpsimd.tensor_copy(take[i][:], idx[:, bass.ds(e, 1), :].rearrange("p a r -> p (a r)")).then_inc(s_take, 1)

            def scatter(e, i):
                pool.wait_ge(s_yv, 2 * e + 2)
                if not first(e):
                    pool.wait_ge(s_add, 16 * RT * e)
                pool.wait_ge(s_ost, 16 * GROUPS)
                for r in range(RT):
                    nc.gpsimd.indirect_dma_start(
                        out=out, out_offset=bass.IndirectOffsetOnAxis(ap=take[i][:, r:r + 1], axis=0),
                        in_=yv[i][:, r, :], in_offset=None, compute_op=ALU.add).then_inc(s_add, 16)

            pool.wait_ge(s_prob, 16)
            pool.wait_ge(s_ost, 16 * GROUPS)
            pool.wait_ge(s_listp, 1)
            pool.wait_ge(s_idx, 1)
            indices(0, 0), gather(0, 0)
            for e in range(EXPERTS):
                if e > 0:
                    pool.wait_ge(s_add, 16 * RT * e)
                if e < EXPERTS - 1:
                    indices(e + 1, (e + 1) % 2), gather(e + 1, (e + 1) % 2)
                scatter(e, e % 2)
            pool.wait_ge(s_add, 16 * RT * EXPERTS)


def kernel(x, L0_tok_W, L0_tok_b, L0_tok_class_token, L0_tok_pos_embed, L0_attn_qkv_weight, L0_attn_proj_weight,
           L0_attn_proj_bias, L0_ffn_Wr, L0_ffn_W1, L0_ffn_b1, L0_ffn_W2, L0_ffn_b2):
    import concourse.bacc as bacc
    from concourse.bass_utils import run_bass_kernel_spmd

    def cols(a):
        return np.ascontiguousarray(np.asarray(a).reshape(-1, 1))

    xp = np.asarray(x).reshape(GROUPS, GROUP, CHANNELS, GRID, PATCH, GRID, PATCH).transpose(0, 2, 4, 6, 1, 3, 5)
    xp = xp.reshape(GROUPS, IN_D, GP)
    wt = np.asarray(L0_tok_W).T
    arrays = {
        "xmain": xp[:, :CHUNKS * 128].reshape(GROUPS, CHUNKS, 128, GP).transpose(0, 2, 1, 3),
        "xtail": xp[:, CHUNKS * 128:],
        "wmain": wt[:CHUNKS * 128].reshape(CHUNKS, 128, HID).transpose(1, 0, 2),
        "wtail": wt[CHUNKS * 128:],
        "cst": constants(),
        "tokb": cols(L0_tok_b),
        "cls": cols(L0_tok_class_token),
        "posT": np.asarray(L0_tok_pos_embed).T,
        "wqkvT": np.asarray(L0_attn_qkv_weight).T,
        "projT": np.asarray(L0_attn_proj_weight).T,
        "projb": cols(L0_attn_proj_bias),
        "wr": np.asarray(L0_ffn_Wr),
        "w1": np.asarray(L0_ffn_W1),
        "b1": np.asarray(L0_ffn_b1).reshape(EXPERTS, FT, 128).transpose(0, 2, 1),
        "w2": np.asarray(L0_ffn_W2).reshape(EXPERTS, FT, 128, HID).transpose(0, 2, 1, 3),
        "b2": np.asarray(L0_ffn_b2),
    }
    arrays = {n: np.ascontiguousarray(a) for n, a in arrays.items()}
    nc = bacc.Bacc("TRN2", target_bir_lowering=False, num_devices=1)
    aps = {n: nc.dram_tensor(n, a.shape, F32, kind="ExternalInput").ap() for n, a in arrays.items()}
    aps["out"] = nc.dram_tensor("out", (TOKENS, HID), F32, kind="ExternalOutput").ap()
    tower(nc, **aps)
    r = run_bass_kernel_spmd(nc, [arrays], core_ids=[0])
    return np.asarray(r.results[0]["out"]).reshape(IMAGES, SEQ, HID)
```

```python
from contextlib import ExitStack

import numpy as np

import concourse.bass as bass
from concourse import mybir

F32 = mybir.dt.float32
F32R = mybir.dt.float32r
F16 = mybir.dt.float16
BF16 = mybir.dt.bfloat16
I32 = mybir.dt.int32
ALU = mybir.AluOpType
ACT = mybir.ActivationFunctionType
AX = mybir.AxisListType

IMAGES, CHANNELS, SIDE, PATCH = 128, 3, 224, 28
GRID = SIDE // PATCH
PATCHES = GRID * GRID
SEQ = PATCHES + 1
HID = 128
IN_D = CHANNELS * PATCH * PATCH
HEAD_D = 8
EXPERTS, FFN, CAP = 8, 512, 1024
TOKENS = IMAGES * SEQ

GROUP = 8
GROUPS = IMAGES // GROUP
GP = GROUP * PATCHES
GT = GROUP * SEQ
HALF_I = GROUP // 2
HT = HALF_I * SEQ
CHUNKS = -(-IN_D // 128)
TAIL = IN_D - (CHUNKS - 1) * 128
LOADS = [(0, 6), (6, 12), (12, CHUNKS - 1)]
UNITS = [(0, 3), (3, 6), (6, 9), (9, 12), (12, 15), (15, 17), (17, CHUNKS)]
NU = len(UNITS)
LAST_UNIT = [1, 3, NU - 1]
POOL_UNITS = (2, 5)
TILE = 104
TPG = GT // TILE
TILES = TOKENS // TILE
SEGS = 16
KPS = TILES // SEGS
SEG = TOKENS // SEGS
ROW = HID + EXPERTS
LO, HI = 64, 16
RT = CAP // 128
FT = FFN // 128
LN_EPS, DEN_EPS = 1e-5, 1e-15

C_CENTRE, C_MEAN, C_HEAD, C_SAME, C_BEFORE, C_ONE, C_IDENT = (128 * n for n in range(7))
C_PCOL = C_IDENT + 128
C_BITS = C_PCOL + 1
C_TILE = C_BITS + 31
C_COLS = C_TILE + EXPERTS * TILES


def constants():
    c = np.zeros((128, C_COLS), np.float32)
    i = np.arange(128)
    c[:, C_CENTRE:C_CENTRE + 128] = np.eye(128) - 1 / 128
    c[:, C_MEAN:C_MEAN + 128] = 1 / 128
    c[:, C_HEAD:C_HEAD + 128] = i[:, None] // HEAD_D == i[None] // HEAD_D
    c[:, C_ONE:C_ONE + 128] = 1
    same = i[:, None] % EXPERTS == i[None] % EXPERTS
    c[:, C_SAME:C_SAME + 128] = same
    c[:, C_BEFORE:C_BEFORE + 128] = same & (i[:, None] // EXPERTS < i[None] // EXPERTS)
    c[:, C_IDENT:C_IDENT + 128] = np.eye(128)
    c[:, C_PCOL] = i
    c[:, C_BITS:C_BITS + 31] = 2.0 ** np.arange(30, -1, -1)
    c[:, C_TILE:] = np.tile(np.arange(TILES), EXPERTS)
    return c


def tower(nc, xmain, xtail, wmain, wtail, cst, tokb, cls, posT, wqkvT, projT, projb, wr, w1, b1, w2, b2, out):
    rows_dram = nc.dram_tensor("rows_dram", (TOKENS, ROW), F32).ap()
    ctx = ExitStack()
    with ctx:
        def sb(stack, name, shape, dt=F32):
            return stack.enter_context(nc.sbuf_tensor(name, shape, dt))

        def sem(name):
            return ctx.enter_context(nc.semaphore(name))

        C = sb(ctx, "C", [128, C_COLS])
        Wr = sb(ctx, "Wr", [128, EXPERTS])
        logits = sb(ctx, "logits", [TILE, KPS, SEGS, EXPERTS])
        idx = sb(ctx, "idx", [128, EXPERTS, RT], I32)
        centre, mean, heads = (C[:, o:o + 128] for o in (C_CENTRE, C_MEAN, C_HEAD))
        same, before, ones, ident = (C[:, o:o + 128] for o in (C_SAME, C_BEFORE, C_ONE, C_IDENT))
        eps_ln = sb(ctx, "eps_ln", [128, 1])
        eps_den = sb(ctx, "eps_den", [128, 1])

        two = range(2)
        A = ExitStack()
        X = sb(A, "X", [128, CHUNKS, GP])
        Xhi = sb(A, "Xhi", [128, CHUNKS, GP], F32R)
        Xlo = sb(A, "Xlo", [128, CHUNKS, GP], F32R)
        W = sb(A, "W", [128, CHUNKS, HID])
        Whi = sb(A, "Whi", [128, CHUNKS, HID], F32R)
        Wlo = sb(A, "Wlo", [128, CHUNKS, HID], F32R)
        Tokb = sb(A, "Tokb", [128, 1])
        Cls = sb(A, "Cls", [128, 1])
        Pos = sb(A, "Pos", [128, SEQ])
        Wqkv = sb(A, "Wqkv", [128, 3 * HID])
        Proj = sb(A, "Proj", [128, HID])
        Projb = sb(A, "Projb", [128, 1])
        Wc1 = sb(A, "Wc1", [128, 4 * HID])
        Wc2 = sb(A, "Wc2", [128, ROW])
        c_col = sb(A, "c_col", [128, 5])
        c_row = sb(A, "c_row", [1, 2 * HID + 1])
        kv_cls = sb(A, "kv_cls", [128, HID + 1])
        hp = sb(A, "hp", [128, GROUP, PATCHES])
        h2 = sb(A, "h2", [128, GROUP, SEQ])
        rows = sb(A, "rows", [TILE, TPG, ROW])
        orow = sb(A, "orow", [TILE, TPG, HID])
        sq2 = sb(A, "sq2", [TILE, TPG, HID])
        ss2 = sb(A, "ss2", [TILE, TPG])
        std2 = sb(A, "std2", [TILE, TPG])
        rstd2 = sb(A, "rstd2", [TILE, TPG])
        sq = sb(A, "sq", [128, 4, HID])
        ss = [sb(A, f"ss{i}", [128, 2]) for i in two]
        std = [sb(A, f"std{i}", [128, 2]) for i in two]
        rstd = [sb(A, f"rstd{i}", [128, 2]) for i in two]
        qk = [sb(A, f"qk{i}", [128, 2, 2 * HID]) for i in two]
        vv = [sb(A, f"vv{i}", [128, 2, HID + 1]) for i in two]
        qT = [sb(A, f"qT{i}", [128, HALF_I, SEQ]) for i in two]
        qs = [sb(A, f"qs{i}", [128, HALF_I, SEQ]) for i in two]
        ksum = [sb(A, f"ksum{i}", [128, HALF_I]) for i in two]
        kvm = [sb(A, f"kvm{i}", [128, HALF_I, HID]) for i in two]
        kvf = [sb(A, f"kvf{i}", [128, HALF_I, HID]) for i in two]
        den = [sb(A, f"den{i}", [128, HT]) for i in two]
        rden = [sb(A, f"rden{i}", [128, HT]) for i in two]
        att = [sb(A, f"att{i}", [128, HT]) for i in two]
        A.close()

        B = ExitStack()
        lt = sb(B, "lt", [128, SEG])
        junk = sb(B, "junk", [128, SEG], BF16)
        ge = sb(B, "ge", [128, SEG])
        eq = sb(B, "eq", [128, SEG])
        scan = sb(B, "scan", [128, SEG])
        slot = sb(B, "slot", [128, SEG])
        rmax = sb(B, "rmax", [128, 1])
        mrow = sb(B, "mrow", [1, EXPERTS])
        mb = sb(B, "mb", [TILE, EXPERTS])
        pex = sb(B, "pex", [TILE, KPS * SEGS, EXPERTS])
        psum_e = sb(B, "psum_e", [TILE, EXPERTS])
        prs = sb(B, "prs", [TILE, EXPERTS])
        prob = sb(B, "prob", [TILE, TILES, EXPERTS])
        cnt = sb(B, "cnt", [128, 1], F16)
        zero = sb(B, "zero", [128, 1])
        cand = sb(B, "cand", [128, 1], I32)
        flip = sb(B, "flip", [128, 1], I32)
        bits = sb(B, "bits", [128, 32], I32)
        same16 = sb(B, "same16", [128, 128], F16)
        tot = sb(B, "tot", [128, 4])
        room = sb(B, "room", [128, 1])
        sloti = sb(B, "sloti", [TILE, EXPERTS, TILES], I32)
        part_i = sb(B, "part_i", [TILE, 2, EXPERTS * TILES], I32)
        part = sb(B, "part", [TILE, 2, EXPERTS * TILES], BF16)
        tile_b = sb(B, "tile_b", [TILE, EXPERTS * TILES], BF16)
        oh_lo = sb(B, "oh_lo", [TILE, EXPERTS, LO, TILES], BF16)
        oh_hi = sb(B, "oh_hi", [TILE, 2, HI, EXPERTS, TILES], BF16)
        val = sb(B, "val", [128, EXPERTS // 2, 2, 2, HI])
        tok = sb(B, "tok", [128, EXPERTS // 2, 2, HI], I32)
        B.close()

        D = ExitStack()
        W1 = [sb(D, f"W1{i}", [128, FFN]) for i in two]
        B1 = [sb(D, f"B1{i}", [128, FT]) for i in two]
        W2 = [sb(D, f"W2{i}", [128, FT, HID]) for i in two]
        B2 = [sb(D, f"B2{i}", [128, HID]) for i in two]
        got = [sb(D, f"got{i}", [128, RT, ROW]) for i in two]
        xe = [sb(D, f"xe{i}", [128, CAP]) for i in two]
        hid = [sb(D, f"hid{i}", [128, FT, CAP]) for i in two]
        yb = [sb(D, f"yb{i}", [128, RT, HID]) for i in two]
        yv = [sb(D, f"yv{i}", [128, RT, HID]) for i in two]
        D.close()

        bank = [ctx.enter_context(nc.psum_tensor(f"bank{i}", [128, 512], F32)) for i in range(8)]
        emb = bank[0]
        za, zb, zq = (bank[1], bank[2]), (bank[3], bank[4]), (bank[5], bank[6])

        s_const, s_wraw, s_pad = sem("const_loaded"), sem("embed_weights_loaded"), sem("padding_zero")
        s_whi, s_wlo = sem("whi_ready"), sem("wlo_ready")
        s_x = [sem(f"x_loaded{n}") for n in range(len(LOADS))]
        s_xt = sem("xtail_loaded")
        s_hi, s_used = sem("xhi_ready"), sem("unit_used")
        s_lo = [sem(f"xlo_ready{u}") for u in range(NU)]
        s_h = sem("h_ready")
        s_set, s_ones, s_wc1 = sem("setup_done"), sem("ones_ready"), sem("wc_psum")
        s_cp, s_ca, s_cv = sem("cls_pe"), sem("cls_act"), sem("cls_dve")
        s_z, s_ss, s_std, s_rstd, s_qk, s_vv = (sem(n) for n in ("qkv_psum", "ss1", "std1", "rstd1", "qk_ready", "vv_ready"))
        s_qt, s_qts, s_kv, s_kvm, s_ks, s_kvf, s_qs = (sem(n) for n in (
            "qt_psum", "qt_ready", "kvprod_psum", "kv_masked", "ksum_ready", "kv_full", "qs_ready"))
        s_num, s_den, s_dens, s_rden, s_att = (sem(n) for n in ("num_psum", "den_psum", "den_ready", "rden_ready", "att_ready"))
        s_pr, s_h2 = sem("proj_psum"), sem("h2_ready")
        s_row, s_tr, s_ss2, s_std2, s_rstd2, s_rows, s_orow, s_log = (sem(n) for n in (
            "rows_psum", "otr_psum", "ss2", "std2", "rstd2", "rows_ready", "orow_ready", "logits_kept"))
        s_rst, s_ost = sem("rows_stored"), sem("out_stored")
        s_ltp, s_lt, s_rmax, s_rmaxt, s_mrow, s_mbp, s_mb, s_pex, s_exp, s_psum, s_tote, s_prs, s_probr = (
            sem(n) for n in ("lt_psum", "lt_ready", "rowmax", "rowmax_t", "mrow", "max_psum", "max_ready", "pex", "exp_ready",
                             "partial_sum", "sum_psum", "rsum", "prob_ready"))
        s_bset, s_cnt, s_tot, s_rej, s_cand = (sem(n) for n in ("search_setup", "counted", "totalled", "rejected", "candidate"))
        s_sel, s_gtot, s_room, s_chosen, s_selt, s_slot, s_slotp = (
            sem(n) for n in ("ties_scanned", "gt_totals", "room", "chosen", "slots_before", "slot_ready", "slot_psum"))
        s_part, s_ohl, s_ohp, s_ohu, s_listp, s_list, s_idx = (
            sem(n) for n in ("slot_parts", "onehot_lo", "onehot_hi_p", "onehot_hi_u", "list_psum", "list_ready", "idx_ready"))
        s_prob = sem("probs_stored")
        s_wc = [sem(f"expert_loaded{i}") for i in two]
        s_got = [sem(f"gathered{i}") for i in two]
        s_xep, s_xe, s_up, s_hid = sem("xe_psum"), sem("xe_ready"), sem("up_psum"), sem("hid_ready")
        s_dn, s_yb, s_yv, s_add = sem("down_psum"), sem("yb_ready"), sem("yv_ready"), sem("added")

        block = ctx.enter_context(nc.Block())

        def first(g):
            return isinstance(g, int) and g == 0

        @block.sync
        def _(sp):
            def load(g, n):
                lo, hi = LOADS[n]
                sp.dma_start(X[:, lo:hi, :], xmain[bass.ds(g, 1), :, lo:hi, :].rearrange("a p c n -> p (a c) n"))\
                    .then_inc(s_x[n], 16)
                if n == len(LOADS) - 1:
                    sp.dma_start(X[:TAIL, CHUNKS - 1, :], xtail[bass.ds(g, 1), :, :].rearrange("a p n -> p (a n)"))\
                        .then_inc(s_xt, 16)

            def reload(g):
                for n, u in enumerate(LAST_UNIT):
                    for v in range(LAST_UNIT[n - 1] + 1 if n else 0, u + 1):
                        sp.wait_ge(s_lo[v], g)
                    load(g, n)

            def store(a):
                sp.wait_ge(s_rows, 2 * a + 2)
                sp.dma_start(rows_dram.rearrange("(g k p) c -> g p k c", p=TILE, k=TPG)[bass.ds(a, 1), :, :, :HID]
                             .rearrange("g p k c -> (g p) k c"), rows[:, :, :HID]).then_inc(s_rst, 16)
                sp.wait_ge(s_orow, 2 * a + 2)
                sp.dma_start(out.rearrange("(g k p) c -> g p k c", p=TILE, k=TPG)[bass.ds(a, 1), :, :, :]
                             .rearrange("g p k c -> (g p) k c"), orow[:]).then_inc(s_ost, 16)

            for lo, hi in LOADS:
                sp.dma_start(W[:, lo:hi, :], wmain[:, lo:hi, :]).then_inc(s_wraw, 16)
            sp.wait_ge(s_pad, 1)
            sp.dma_start(W[:TAIL, CHUNKS - 1, :], wtail).then_inc(s_wraw, 16)
            load(0, 0)
            for dst, src in ((C[:], cst), (Wr[:], wr), (Tokb[:], tokb), (Cls[:], cls), (Pos[:], posT),
                             (Wqkv[:], wqkvT), (Proj[:], projT), (Projb[:], projb)):
                sp.dma_start(dst, src).then_inc(s_const, 16)
            load(0, 1), load(0, 2)
            reload(1)
            reload(2)
            with sp.Fori(3, GROUPS) as g:
                reload(g)
                store(g - 3)
            for a in range(GROUPS - 3, GROUPS):
                store(a)

            sp.wait_ge(s_probr, 1)
            sp.wait_ge(s_rst, 16 * GROUPS)
            sp.dma_start(rows_dram.rearrange("(u p) c -> p u c", p=TILE)[:, :, HID:ROW], prob[:]).then_inc(s_prob, 16)

            def weights(e, i):
                sp.dma_start(W1[i][:], w1[bass.ds(e, 1), :, :].rearrange("a p n -> p (a n)")).then_inc(s_wc[i], 16)
                sp.dma_start(B1[i][:], b1[bass.ds(e, 1), :, :].rearrange("a p n -> p (a n)")).then_inc(s_wc[i], 16)
                sp.dma_start(W2[i][:], w2[bass.ds(e, 1), :, :, :].rearrange("a p f n -> p (a f) n")).then_inc(s_wc[i], 16)
                sp.dma_start(B2[i][:], b2[bass.ds(e, 1), :].broadcast_to([128, HID])).then_inc(s_wc[i], 16)

            sp.wait_ge(s_prob, 16)
            sp.wait_ge(s_listp, 1)
            sp.wait_ge(s_idx, 1)
            weights(0, 0)
            weights(1, 1)
            with sp.Fori(1, EXPERTS // 2) as j:
                for i in two:
                    sp.wait_ge(s_yv, 4 * j + 2 * i - 2)
                    weights(j * 2 + i, i)

        @block.tensor
        def _(pe):
            def embed(g, lo, hi):
                for u in range(lo, hi):
                    pe.wait_ge(s_lo[u], g + 1)
                    if u == 0 and not first(g):
                        pe.wait_ge(s_h, g)
                    for c in range(*UNITS[u]):
                        nc.tensor.matmul(emb[:], Whi[:, c, :], Xhi[:, c, :], start=(c == 0), stop=False)
                        nc.tensor.matmul(emb[:], Whi[:, c, :], Xlo[:, c, :], start=False, stop=False)
                        last = nc.tensor.matmul(emb[:], Wlo[:, c, :], Xhi[:, c, :], start=False, stop=(c == CHUNKS - 1))
                    last.then_inc(s_used, 1)

            def qkv(a, i):
                pe.wait_ge(s_h, a + 1)
                if not first(a):
                    pe.wait_ge(s_orow, 2 * a)
                for pair, z in enumerate((za[i], zb[i])):
                    at = HALF_I * i + 2 * pair
                    nc.tensor.matmul(z[:], hp[:, at:at + 2, :].rearrange("p a b -> p (a b)"), Wc1[:],
                                     start=True, stop=True).then_inc(s_z, 1)

            def q_columns(a, i):
                pe.wait_ge(s_qk, 4 * a + 2 * i + 2)
                if not first(a):
                    pe.wait_ge(s_rows, 2 * a)
                for pair in two:
                    last = nc.tensor.transpose(zq[i][:, HID * pair:HID * (pair + 1)], qk[i][:, pair, :HID], ident)
                last.then_inc(s_qt, 1)

            def kvprod(a, i):
                pe.wait_ge(s_vv, 4 * a + 2 * i + 2)
                for im in range(HALF_I):
                    r = slice(64 * (im % 2), 64 * (im % 2) + 64)
                    dst = (za, zb)[im % 2][i]
                    last = nc.tensor.matmul(dst[:, 129 * (im // 2):129 * (im // 2) + 129], qk[i][r, im // 2, HID:],
                                            vv[i][r, im // 2, :], start=True, stop=True)
                last.then_inc(s_kv, 1)

            def attend(a, i):
                pe.wait_ge(s_kvf, 2 * a + i + 1)
                pe.wait_ge(s_qts, 2 * a + i + 1)
                for im in range(HALF_I):
                    last = nc.tensor.matmul(zq[i][:, SEQ * im:SEQ * (im + 1)], kvf[i][:, im, :], qT[i][:, im, :],
                                            start=True, stop=True)
                last.then_inc(s_num, 1)
                pe.wait_ge(s_qs, 2 * a + i + 1)
                nc.tensor.matmul(za[i][:, :HT], heads, qs[i][:], start=True, stop=True).then_inc(s_den, 1)

            def project(a, i):
                pe.wait_ge(s_att, 2 * a + i + 1)
                nc.tensor.matmul(zb[i][:, :HT], Proj[:], att[i][:], start=True, stop=True).then_inc(s_pr, 1)

            def to_rows(a):
                pe.wait_ge(s_h2, 4 * a + 4)
                flat = h2[:].rearrange("p a b -> p (a b)")
                for k in range(TPG):
                    last = nc.tensor.matmul(zq[k // 3][:TILE, ROW * (k % 3):ROW * (k % 3 + 1)],
                                            flat[:, TILE * k:TILE * (k + 1)], Wc2[:], start=True, stop=True)
                    if k in (2, TPG - 1):
                        last.then_inc(s_row, 1)
                for k in range(TPG):
                    last = nc.tensor.transpose(za[k // 4][:TILE, HID * (k % 4):HID * (k % 4 + 1)],
                                               flat[:, TILE * k:TILE * (k + 1)], ident)
                    if k in (3, TPG - 1):
                        last.then_inc(s_tr, 1)

            pe.wait_ge(s_wlo, 1)
            embed(0, 0, 2)
            pe.wait_ge(s_set, 1)
            nc.tensor.matmul(za[1][:, :3 * HID], centre, Wqkv[:], start=True, stop=True)
            nc.tensor.matmul(zb[1][:, :EXPERTS], centre, Wr[:], start=True, stop=True).then_inc(s_wc1, 1)
            nc.tensor.matmul(za[0][:, 0:1], centre, c_col[:, 0:1], start=True, stop=True).then_inc(s_cp, 1)
            pe.wait_ge(s_ca, 1)
            nc.tensor.matmul(zb[0][:, 0:1], mean, c_col[:, 1:2], start=True, stop=True).then_inc(s_cp, 1)
            pe.wait_ge(s_cv, 2)
            nc.tensor.matmul(za[0][0:1, 0:256], c_col[:, 4:5], Wqkv[:, HID:], start=True, stop=True)
            nc.tensor.matmul(zq[0][:, 0:1], Wqkv[:, :HID], c_col[:, 4:5], start=True, stop=True).then_inc(s_cp, 1)
            pe.wait_ge(s_ca, 4)
            nc.tensor.matmul(zb[0][:, 0:HID + 1], c_row[:, 0:HID], c_row[:, HID:], start=True, stop=True).then_inc(s_cp, 1)

            embed(0, 2, NU)
            pe.wait_ge(s_cv, 5)

            def both(g, a):
                embed(g, 0, 1)
                qkv(a, 0), qkv(a, 1)
                embed(g, 1, 2)
                q_columns(a, 0), kvprod(a, 0), q_columns(a, 1), kvprod(a, 1)
                embed(g, 2, 4)
                attend(a, 0), attend(a, 1)
                embed(g, 4, 6)
                project(a, 0), project(a, 1)
                embed(g, 6, NU)
                to_rows(a)

            both(1, 0)
            with pe.Fori(2, GROUPS) as g:
                both(g, g - 1)
            for step in (qkv, q_columns, kvprod, attend, project):
                step(GROUPS - 1, 0), step(GROUPS - 1, 1)
            to_rows(GROUPS - 1)

            pe.wait_ge(s_rows, 2 * GROUPS)
            pe.wait_ge(s_orow, 2 * GROUPS)
            pe.wait_ge(s_log, GROUPS)
            for k in range(KPS):
                last = nc.tensor.transpose(bank[k // 4][:, TILE * (k % 4):TILE * (k % 4 + 1)], logits[:, k, :, :].rearrange("p s e -> p (s e)"), ident[:TILE, :TILE])
            last.then_inc(s_ltp, 1)
            pe.wait_ge(s_rmax, 1)
            nc.tensor.transpose(bank[2][:1, :128], rmax[:], ident).then_inc(s_rmaxt, 1)
            pe.wait_ge(s_mrow, 1)
            nc.tensor.matmul(bank[3][:TILE, :EXPERTS], ones[:1, :TILE], mrow[:], start=True, stop=True).then_inc(s_mbp, 1)

            def total(n):
                pe.wait_ge(s_cnt, n + 1)
                nc.tensor.matmul(bank[5 + n % 2][:, 0:1], same16[:], cnt[:], start=True, stop=True).then_inc(s_tot, 1)

            for n in range(2):
                total(n)
            pe.wait_ge(s_psum, 1)
            nc.tensor.matmul(bank[4][:TILE, :EXPERTS], ones[:TILE, :TILE], psum_e[:], start=True, stop=True).then_inc(s_tote, 1)
            for n in range(2, 32):
                total(n)
            pe.wait_ge(s_sel, 1)
            nc.tensor.matmul(bank[5][:, 0:1], same, tot[:, 0:1], start=True, stop=True)
            nc.tensor.matmul(bank[5][:, 1:2], before, tot[:, 1:2], start=True, stop=True).then_inc(s_gtot, 1)
            pe.wait_ge(s_chosen, 1)
            nc.tensor.matmul(bank[6][:, 0:1], before, scan[:, SEG - 1:SEG], start=True, stop=True).then_inc(s_selt, 1)
            pe.wait_ge(s_slot, 1)
            for k in range(KPS):
                last = nc.tensor.transpose(bank[k // 4][:TILE, 128 * (k % 4):128 * (k % 4 + 1)],
                                           slot[:, TILE * k:TILE * (k + 1)], ident)
            last.then_inc(s_slotp, 1)
            pe.wait_ge(s_ohl, LO)
            pe.wait_ge(s_ohp, HI)
            pe.wait_ge(s_ohu, HI)
            for pair in range(EXPERTS // 2):
                for u in range(TILES):
                    last = nc.tensor.matmul(bank[7][:, 64 * pair:64 * (pair + 1)],
                                            oh_lo[:, 2 * pair:2 * pair + 2, :, u].rearrange("p e a -> p (e a)"),
                                            oh_hi[:, :, :, 2 * pair:2 * pair + 2, u].rearrange("p v a e -> p v e a"),
                                            start=(pair == 0 and u == 0), stop=(u == TILES - 1), skip_group_check=True)
            last.then_inc(s_listp, 1)

            def run_expert(j, i):
                n = 2 * j + i
                start = first(j) and i == 0
                pe.wait_ge(s_got[i], 16 * RT * (j + 1))
                if not start:
                    pe.wait_ge(s_xe, 2 * n)
                for r in range(RT):
                    last = nc.tensor.transpose(bank[r // 4][:, 128 * (r % 4):128 * (r % 4 + 1)], got[i][:, r, :HID], ident)
                    if r % 4 == 3:
                        last.then_inc(s_xep, 1)
                pe.wait_ge(s_wc[i], 64 * (j + 1))
                for half in two:
                    pe.wait_ge(s_xe, 2 * n + half + 1)
                    for f in range(FT):
                        m = FT * half + f
                        if not start or m >= 4:
                            pe.wait_ge(s_hid, 8 * n + m - 3)
                        nc.tensor.matmul(bank[2 + m % 4][:], W1[i][:, 128 * f:128 * (f + 1)],
                                         xe[i][:, 512 * half:512 * (half + 1)], start=True, stop=True).then_inc(s_up, 1)
                for r in range(RT):
                    if r % 4 == 0:
                        pe.wait_ge(s_hid, 8 * n + r + 4)
                        if not start:
                            pe.wait_ge(s_yb, 2 * n + r // 4 - 1)
                    for f in range(FT):
                        last = nc.tensor.matmul(bank[6 + r // 4][:, 128 * (r % 4):128 * (r % 4 + 1)],
                                                hid[i][:, f, 128 * r:128 * (r + 1)], W2[i][:, f, :],
                                                start=(f == 0 and r % 4 == 0), stop=(f == FT - 1), skip_group_check=True)
                    if r % 4 == 3:
                        last.then_inc(s_dn, 1)

            run_expert(0, 0)
            run_expert(0, 1)
            with pe.Fori(1, EXPERTS // 2) as j:
                run_expert(j, 0)
                run_expert(j, 1)

        @block.scalar
        def _(act):
            def round_unit(g, u):
                lo, hi = UNITS[u]
                for n, (a, b) in enumerate(LOADS):
                    if lo == a:
                        act.wait_ge(s_x[n], 16 * g + 16)
                if hi == CHUNKS:
                    act.wait_ge(s_xt, 16 * g + 16)
                if not first(g):
                    act.wait_ge(s_used, NU * (g - 1) + u + 1)
                nc.scalar.activation(Xhi[:, lo:hi, :], X[:, lo:hi, :], ACT.Copy).then_inc(s_hi, 1)

            def squares(a, i):
                for pair, z in enumerate((za[i], zb[i])):
                    act.wait_ge(s_z, 4 * a + 2 * i + pair + 1)
                    nc.scalar.activation(sq[:, 2 * i + pair], z[:, :HID], ACT.Square, accum_out=ss[i][:, pair:pair + 1]).then_inc(s_ss, 1)
                act.wait_ge(s_ss, 4 * a + 2 * i + 2)
                nc.scalar.activation(std[i][:], ss[i][:], ACT.Sqrt, bias=eps_ln[:], scale=1 / HID).then_inc(s_std, 1)

            def values(a, i):
                for pair, z in enumerate((za[i], zb[i])):
                    act.wait_ge(s_qk, 4 * a + 2 * i + pair + 1)
                    nc.scalar.activation(vv[i][:, pair, :HID], z[:, 3 * HID:], ACT.Copy,
                                         scale=rstd[i][:, pair:pair + 1]).then_inc(s_vv, 1)

            def q_columns(a, i):
                act.wait_ge(s_qt, 2 * a + i + 1)
                nc.scalar.activation(qT[i][:, :, 1:], zq[i][:, :2 * HID].rearrange("p (a b) -> p a b", b=PATCHES),
                                     ACT.Copy).then_inc(s_qts, 1)

            def denominator(a, i):
                act.wait_ge(s_den, 2 * a + i + 1)
                nc.scalar.activation(den[i][:], za[i][:, :HT], ACT.Identity, bias=eps_den[:]).then_inc(s_dens, 1)

            TRIPS = ((0, 3), (3, TPG))

            def row_squares(a):
                for n, (lo, hi) in enumerate(TRIPS):
                    act.wait_ge(s_row, 2 * a + n + 1)
                    for k in range(lo, hi):
                        nc.scalar.activation(sq2[:, k], zq[n][:TILE, ROW * (k - lo):ROW * (k - lo) + HID], ACT.Square,
                                             accum_out=ss2[:, k:k + 1]).then_inc(s_ss2, 1)
                act.wait_ge(s_ss2, TPG * a + TPG)
                nc.scalar.activation(std2[:], ss2[:], ACT.Sqrt, bias=eps_ln[:TILE], scale=1 / HID).then_inc(s_std2, 1)

            def to_rows(a):
                for n, (lo, hi) in enumerate(((0, 4), (4, TPG))):
                    act.wait_ge(s_tr, 2 * a + n + 1)
                    if n == 0 and not first(a):
                        act.wait_ge(s_ost, 16 * a)
                    nc.scalar.activation(orow[:, lo:hi, :], za[n][:TILE, :HID * (hi - lo)].rearrange("p (k c) -> p k c", c=HID),
                                         ACT.Copy).then_inc(s_orow, 1)
                act.wait_ge(s_rstd2, a + 1)
                if not first(a):
                    act.wait_ge(s_rst, 16 * a)
                    act.wait_ge(s_log, a)
                for n, (lo, hi) in enumerate(TRIPS):
                    for k in range(lo, hi):
                        last = nc.scalar.activation(rows[:, k, :], zq[n][:TILE, ROW * (k - lo):ROW * (k - lo + 1)], ACT.Copy,
                                                    scale=rstd2[:, k:k + 1])
                    last.then_inc(s_rows, 1)

            def group(a, more):
                def rounding(*units):
                    for u in units if more else ():
                        round_unit(a + 2, u)

                rounding(0)
                squares(a, 0), squares(a, 1)
                values(a, 0), values(a, 1)
                rounding(1)
                q_columns(a, 0), q_columns(a, 1)
                rounding(2, 3)
                denominator(a, 0), denominator(a, 1)
                rounding(4, 5, 6)
                row_squares(a)
                to_rows(a)

            act.wait_ge(s_wraw, 16 * (len(LOADS) + 1))
            nc.scalar.activation(Whi[:], W[:], ACT.Copy).then_inc(s_whi, 1)
            round_unit(0, 0), round_unit(0, 1)

            act.wait_ge(s_ones, 1)
            act.wait_ge(s_cp, 1)
            nc.scalar.activation(c_col[:, 1:2], za[0][:, 0:1], ACT.Square).then_inc(s_ca, 1)
            act.wait_ge(s_cp, 2)
            nc.scalar.activation(c_col[:, 2:3], zb[0][:, 0:1], ACT.Sqrt, bias=eps_ln[:]).then_inc(s_ca, 1)
            act.wait_ge(s_cp, 3)
            nc.scalar.activation(c_row[:, :HID], za[0][:1, :HID], ACT.Relu).then_inc(s_ca, 1)
            nc.scalar.activation(c_row[:, HID:2 * HID], za[0][:1, HID:256], ACT.Copy).then_inc(s_ca, 1)

            for u in range(2, NU):
                round_unit(0, u)
            for u in range(NU):
                round_unit(1, u)
            group(0, True)
            with act.Fori(1, GROUPS - 2) as a:
                group(a, True)
            group(GROUPS - 2, False)
            group(GROUPS - 1, False)

            act.wait_ge(s_pex, 1)
            nc.scalar.activation(pex[:], pex[:], ACT.Exp).then_inc(s_exp, 1)

            def hidden(j, i):
                n = 2 * j + i
                act.wait_ge(s_wc[i], 64 * (j + 1))
                for m in range(2 * FT):
                    half, f = m // FT, m % FT
                    act.wait_ge(s_up, 8 * n + m + 1)
                    if m == 0 and not first(j):
                        act.wait_ge(s_dn, 2 * n - 2)
                    nc.scalar.activation(hid[i][:, f, 512 * half:512 * (half + 1)], bank[2 + m % 4][:], ACT.Gelu,
                                         bias=B1[i][:, f:f + 1]).then_inc(s_hid, 1)

            hidden(0, 0)
            hidden(0, 1)
            with act.Fori(1, EXPERTS // 2) as j:
                hidden(j, 0)
                hidden(j, 1)

        @block.vector
        def _(dve):
            def low_unit(g, u):
                lo, hi = UNITS[u]
                dve.wait_ge(s_hi, NU * g + u + 1)
                nc.vector.tensor_tensor(Xlo[:, lo:hi, :], X[:, lo:hi, :], Xhi[:, lo:hi, :].bitcast(F32),
                                        ALU.subtract).then_inc(s_lo[u], 1)

            def evacuate(g):
                if not first(g):
                    dve.wait_ge(s_h2, 4 * g)
                dve.wait_ge(s_used, NU * g + NU)
                nc.vector.scalar_tensor_tensor(
                    out=hp[:], in0=emb[:].rearrange("p (b n) -> p b n", b=GROUP), scalar=Tokb[:],
                    in1=Pos[:, 1:].unsqueeze(1).broadcast_to([128, GROUP, PATCHES]), op0=ALU.add, op1=ALU.mult).then_inc(s_h, 1)

            def norm_qk(a, i):
                dve.wait_ge(s_std, 2 * a + i + 1)
                nc.vector.reciprocal(rstd[i][:], std[i][:]).then_inc(s_rstd, 1)
                dve.wait_ge(s_rstd, 2 * a + i + 1)
                for pair, z in enumerate((za[i], zb[i])):
                    nc.vector.tensor_scalar(qk[i][:, pair, :], z[:, HID:3 * HID], rstd[i][:, pair:pair + 1], 0.0,
                                            ALU.mult, ALU.max).then_inc(s_qk, 1)

            def mask(a, i):
                dve.wait_ge(s_kv, 2 * a + i + 1)
                for n, z in enumerate((za, zb)):
                    kv = z[i][:, :258].rearrange("p (b c) -> p b c", b=2)
                    last = nc.vector.tensor_tensor(kvm[i][:, n::2, :], kv[:, :, :HID],
                                                   heads.unsqueeze(1).broadcast_to([128, 2, HID]), ALU.mult)
                last.then_inc(s_kvm, 1)
                for n, z in enumerate((za, zb)):
                    kv = z[i][:, :258].rearrange("p (b c) -> p b c", b=2)
                    last = nc.vector.tensor_scalar(ksum[i][:, n::2].unsqueeze(2), kv[:, :, HID:], kv_cls[:, HID:], None, ALU.add)
                last.then_inc(s_ks, 1)

            def attention(a, i):
                dve.wait_ge(s_dens, 2 * a + i + 1)
                nc.vector.reciprocal(rden[i][:], den[i][:]).then_inc(s_rden, 1)
                dve.wait_ge(s_rden, 2 * a + i + 1)
                dve.wait_ge(s_num, 2 * a + i + 1)
                nc.vector.tensor_tensor(att[i][:], zq[i][:, :HT], rden[i][:], ALU.mult).then_inc(s_att, 1)

            def residual(a, i):
                dve.wait_ge(s_pr, 2 * a + i + 1)
                own = slice(HALF_I * i, HALF_I * (i + 1))
                pr = zb[i][:, :HT].rearrange("p (a b) -> p a b", b=SEQ)
                nc.vector.scalar_tensor_tensor(out=h2[:, own, 1:], in0=pr[:, :, 1:], scalar=Projb[:], in1=hp[:, own, :],
                                               op0=ALU.add, op1=ALU.add).then_inc(s_h2, 1)
                nc.vector.scalar_tensor_tensor(out=h2[:, own, 0], in0=pr[:, :, 0], scalar=Projb[:],
                                               in1=c_col[:, 0:1].broadcast_to([128, HALF_I]),
                                               op0=ALU.add, op1=ALU.add).then_inc(s_h2, 1)

            def norm_rows(a):
                dve.wait_ge(s_std2, a + 1)
                nc.vector.reciprocal(rstd2[:], std2[:]).then_inc(s_rstd2, 1)

            def group(a, more, embedding):
                def low(*units):
                    for u in units if more else ():
                        low_unit(a + 2, u)

                low(0)
                norm_qk(a, 0), norm_qk(a, 1)
                low(1)
                mask(a, 0), mask(a, 1)
                low(3)
                attention(a, 0), attention(a, 1)
                low(4)
                residual(a, 0), residual(a, 1)
                if embedding:
                    evacuate(a + 1)
                low(6)
                norm_rows(a)

            nc.vector.memset(W[:, CHUNKS - 1, :], 0.0)
            nc.vector.memset(X[:, CHUNKS - 1, :], 0.0).then_inc(s_pad, 1)
            nc.vector.memset(eps_ln[:], LN_EPS)
            nc.vector.memset(eps_den[:], DEN_EPS)
            nc.vector.memset(c_row[:, 2 * HID:], 1.0)
            for i in two:
                last = nc.vector.memset(vv[i][:, :, HID:], 1.0)
            last.then_inc(s_ones, 1)
            dve.wait_ge(s_whi, 1)
            nc.vector.tensor_tensor(Wlo[:], W[:], Whi[:].bitcast(F32), ALU.subtract).then_inc(s_wlo, 1)
            low_unit(0, 0), low_unit(0, 1)

            dve.wait_ge(s_const, 16 * 8)
            nc.vector.tensor_tensor(c_col[:, 0:1], Cls[:], Pos[:, 0:1], ALU.mult).then_inc(s_set, 1)
            dve.wait_ge(s_ca, 2)
            nc.vector.reciprocal(c_col[:, 3:4], c_col[:, 2:3]).then_inc(s_cv, 1)
            dve.wait_ge(s_cv, 1)
            nc.vector.tensor_tensor(c_col[:, 4:5], za[0][:, 0:1], c_col[:, 3:4], ALU.mult).then_inc(s_cv, 1)
            dve.wait_ge(s_wc1, 1)
            for w in (Wc1, Wc2):
                nc.vector.tensor_copy(w[:, :HID], centre)
            nc.vector.tensor_copy(Wc1[:, HID:], za[1][:, :3 * HID])
            nc.vector.tensor_copy(Wc2[:, HID:], zb[1][:, :EXPERTS]).then_inc(s_cv, 1)
            dve.wait_ge(s_cp, 4)
            nc.vector.tensor_tensor(kv_cls[:, :HID], zb[0][:, :HID], heads, ALU.mult)
            nc.vector.tensor_copy(kv_cls[:, HID:], zb[0][:, HID:HID + 1]).then_inc(s_cv, 1)
            for i in two:
                last = nc.vector.tensor_scalar(qT[i][:, :, 0], zq[0][:, 0:1].broadcast_to([128, HALF_I]), 0.0, None, ALU.max)
            last.then_inc(s_cv, 1)
            dve.wait_ge(s_cv, 5)

            low_unit(0, 3), low_unit(0, 4), low_unit(0, 6)
            for u in (0, 1, 3, 4):
                low_unit(1, u)
            evacuate(0)
            low_unit(1, 6)
            with dve.Fori(0, GROUPS - 2) as a:
                group(a, True, True)
            group(GROUPS - 2, False, True)
            group(GROUPS - 1, False, False)

            dve.wait_ge(s_rst, 16 * GROUPS)
            dve.wait_ge(s_ost, 16 * GROUPS)
            dve.wait_ge(s_orow, 2 * GROUPS)
            nc.vector.tensor_copy(bits[:, :31], C[:, C_BITS:C_BITS + 31])
            nc.vector.memset(zero[:], 0.0)
            nc.vector.tensor_copy(same16[:], same).then_inc(s_bset, 1)
            dve.wait_ge(s_ltp, 1)
            nc.vector.tensor_copy(lt[:, :4 * TILE], bank[0][:, :4 * TILE])
            nc.vector.tensor_copy(lt[:, 4 * TILE:], bank[1][:, :TILE]).then_inc(s_lt, 1)
            dve.wait_ge(s_lt, 1)
            dve.wait_ge(s_bset, 1)
            nc.vector.reduce_max(rmax[:], lt[:], axis=AX.X).then_inc(s_rmax, 1)
            dve.wait_ge(s_rmaxt, 1)
            nc.vector.reduce_max(mrow[:], bank[2][:1, :128].rearrange("p (s e) -> p e s", e=EXPERTS), axis=AX.X).then_inc(s_mrow, 1)
            dve.wait_ge(s_mbp, 1)
            nc.vector.tensor_copy(mb[:], bank[3][:TILE, :EXPERTS]).then_inc(s_mb, 1)
            dve.wait_ge(s_mb, 1)
            nc.vector.tensor_tensor(pex[:], logits[:].rearrange("p k s e -> p (k s) e"), mb[:].unsqueeze(1).broadcast_to([TILE, TILES, EXPERTS]),
                                    ALU.subtract).then_inc(s_pex, 1)

            def count(n, threshold):
                nc.vector.tensor_scalar(junk[:], lt[:], threshold, None, ALU.is_ge, ALU.add, accum_out=cnt[:]).then_inc(s_cnt, 1)

            BIT = [1 << (30 - n) for n in range(31)]
            count(0, 0.0)
            dve.wait_ge(s_tot, 1)
            nc.vector.tensor_scalar(flip[:], bank[5][:, 0:1], float(CAP), -1.0, ALU.is_lt, ALU.mult).then_inc(s_rej, 1)
            dve.wait_ge(s_rej, 1)
            nc.vector.tensor_scalar(cand[:], flip[:], BIT[0], None, ALU.bitwise_xor).then_inc(s_cand, 1)
            for n in range(1, 32):
                dve.wait_ge(s_cand, n)
                count(n, cand[:].bitcast(F32))
                if n == 1:
                    dve.wait_ge(s_exp, 1)
                    nc.vector.reduce_sum(psum_e[:], pex[:].rearrange("p u e -> p e u"), axis=AX.X).then_inc(s_psum, 1)
                    dve.wait_ge(s_tote, 1)
                    nc.vector.reciprocal(prs[:], bank[4][:TILE, :EXPERTS]).then_inc(s_prs, 1)
                    dve.wait_ge(s_prs, 1)
                    nc.vector.tensor_tensor(prob[:].rearrange("p (s k) e -> p k s e", k=KPS),
                                            pex[:].rearrange("p (k s) e -> p k s e", k=KPS),
                                            prs[:].unsqueeze(1).unsqueeze(1).broadcast_to([TILE, KPS, SEGS, EXPERTS]), ALU.mult).then_inc(s_probr, 1)
                dve.wait_ge(s_tot, n + 1)
                nc.vector.tensor_scalar(flip[:], bank[5 + n % 2][:, 0:1], float(CAP), float(BIT[n - 1]), ALU.is_lt, ALU.mult)\
                    .then_inc(s_rej, 1)
                dve.wait_ge(s_rej, n + 1)
                if n < 31:
                    nc.vector.scalar_tensor_tensor(out=cand[:], in0=cand[:], scalar=BIT[n], in1=flip[:],
                                                   op0=ALU.bitwise_xor, op1=ALU.bitwise_xor).then_inc(s_cand, 1)
                else:
                    nc.vector.tensor_tensor(cand[:], cand[:], flip[:], ALU.bitwise_xor).then_inc(s_cand, 1)
            dve.wait_ge(s_cand, 32)

            T = cand[:].bitcast(F32)
            nc.vector.tensor_scalar(ge[:], lt[:], T, None, ALU.is_gt, ALU.add, accum_out=tot[:, 0:1])
            nc.vector.tensor_scalar(eq[:], lt[:], T, None, ALU.is_equal, ALU.add, accum_out=tot[:, 1:2]).then_inc(s_sel, 1)
            dve.wait_ge(s_sel, 1)
            nc.vector.tensor_tensor_scan(scan[:], eq[:], eq[:], 0.0, ALU.add, ALU.max).then_inc(s_sel, 1)
            dve.wait_ge(s_gtot, 1)
            nc.vector.tensor_scalar(tot[:, 2:3], bank[5][:, 0:1], -1.0, float(CAP), ALU.mult, ALU.add).then_inc(s_sel, 1)
            dve.wait_ge(s_sel, 3)
            nc.vector.tensor_tensor(room[:], tot[:, 2:3], bank[5][:, 1:2], ALU.subtract).then_inc(s_room, 1)
            dve.wait_ge(s_room, 1)
            nc.vector.scalar_tensor_tensor(out=eq[:], in0=scan[:], scalar=room[:], in1=eq[:],
                                           op0=ALU.is_le, op1=ALU.mult).then_inc(s_room, 1)
            dve.wait_ge(s_room, 2)
            nc.vector.tensor_tensor(ge[:], ge[:], eq[:], ALU.add).then_inc(s_room, 1)
            dve.wait_ge(s_room, 3)
            nc.vector.tensor_tensor_scan(scan[:], ge[:], ge[:], 0.0, ALU.add, ALU.max).then_inc(s_chosen, 1)
            dve.wait_ge(s_chosen, 1)
            dve.wait_ge(s_selt, 1)
            nc.vector.tensor_copy(room[:], bank[6][:, 0:1]).then_inc(s_room, 1)
            dve.wait_ge(s_room, 4)
            nc.vector.scalar_tensor_tensor(out=scan[:], in0=scan[:], scalar=room[:], in1=ge[:],
                                           op0=ALU.add, op1=ALU.mult).then_inc(s_room, 1)
            dve.wait_ge(s_room, 5)
            nc.vector.tensor_scalar(slot[:], scan[:], -1.0, None, ALU.add).then_inc(s_slot, 1)
            dve.wait_ge(s_slotp, 1)
            for n, (lo, hi) in enumerate(((0, 4), (4, KPS))):
                last = nc.vector.tensor_copy(sloti[:].rearrange("p e (s k) -> p k s e", k=KPS)[:, lo:hi],
                                             bank[n][:TILE, :128 * (hi - lo)].rearrange("p (k s e) -> p k s e", s=SEGS, e=EXPERTS))
            last.then_inc(s_part, 1)
            dve.wait_ge(s_part, 1)
            nc.vector.tensor_scalar(part_i[:, 0, :], sloti[:].rearrange("p e u -> p (e u)"), LO - 1, None, ALU.bitwise_and)
            nc.vector.tensor_scalar(part_i[:, 1, :], sloti[:].rearrange("p e u -> p (e u)"), LO.bit_length() - 1, None, ALU.arith_shift_right)
            nc.vector.tensor_copy(tile_b[:], C[:TILE, C_TILE:]).then_inc(s_part, 1)
            dve.wait_ge(s_part, 2)
            nc.vector.tensor_copy(part[:], part_i[:]).then_inc(s_part, 1)
            dve.wait_ge(s_part, 3)
            for v in range(LO):
                nc.vector.tensor_scalar(oh_lo[:, :, v, :],
                                        part[:, 0, :].rearrange("p (e u) -> p e u", e=EXPERTS), float(v), None, ALU.is_equal).then_inc(s_ohl, 1)
            for v in range(HI):
                nc.vector.tensor_scalar(oh_hi[:, 0, v].rearrange("p e u -> p (e u)"), part[:, 1, :], float(v), C[:TILE, C_PCOL:C_PCOL + 1],
                                        ALU.is_equal, ALU.mult).then_inc(s_ohp, 1)
            for v in range(HI):
                nc.vector.scalar_tensor_tensor(out=oh_hi[:, 1, v].rearrange("p e u -> p (e u)"), in0=part[:, 1, :], scalar=float(v), in1=tile_b[:],
                                               op0=ALU.is_equal, op1=ALU.mult).then_inc(s_ohu, 1)
            dve.wait_ge(s_listp, 1)
            nc.vector.tensor_copy(val[:].rearrange("p a v e h -> p (a v e h)"), bank[7][:, :256]).then_inc(s_list, 1)
            dve.wait_ge(s_list, 1)
            nc.vector.scalar_tensor_tensor(out=tok[:], in0=val[:, :, 1], scalar=float(TILE), in1=val[:, :, 0],
                                           op0=ALU.mult, op1=ALU.add).then_inc(s_list, 1)
            dve.wait_ge(s_list, 2)
            dve.wait_ge(s_prob, 16)
            for e2 in two:
                for h2_ in two:
                    last = nc.vector.tensor_copy(
                        idx[64 * h2_:64 * h2_ + 64].rearrange("p (a e) r -> p a e r", e=2)[:, :, e2, :],
                        tok[64 * e2:64 * e2 + 64].rearrange("p a e (r h) -> p a e r h", h=2)[:, :, e2, :, h2_])
            last.then_inc(s_idx, 1)

            def inputs(j, i):
                n = 2 * j + i
                for half in two:
                    dve.wait_ge(s_xep, 2 * n + half + 1)
                    nc.vector.tensor_copy(xe[i][:, 512 * half:512 * (half + 1)], bank[half][:]).then_inc(s_xe, 1)

            def outputs(j, i):
                n = 2 * j + i
                for half in two:
                    dve.wait_ge(s_dn, 2 * n + half + 1)
                    dve.wait_ge(s_wc[i], 64 * (j + 1))
                    r = slice(4 * half, 4 * half + 4)
                    nc.vector.tensor_tensor(yb[i][:, r, :], bank[6 + half][:].rearrange("p (r c) -> p r c", c=HID),
                                            B2[i][:].unsqueeze(1).broadcast_to([128, 4, HID]), ALU.add).then_inc(s_yb, 1)
                    dve.wait_ge(s_yb, 2 * n + half + 1)
                    if not first(j):
                        dve.wait_ge(s_add, 16 * RT * (n - 1))
                    e = HID + n
                    nc.vector.tensor_tensor(yv[i][:, r, :], yb[i][:, r, :],
                                            got[i][:, r, bass.ds(e, 1)].broadcast_to([128, 4, HID]), ALU.mult).then_inc(s_yv, 1)

            inputs(0, 0), outputs(0, 0), inputs(0, 1), outputs(0, 1)
            with dve.Fori(1, EXPERTS // 2) as j:
                inputs(j, 0), outputs(j, 0), inputs(j, 1), outputs(j, 1)

        @block.gpsimd
        def _(pool):
            def low_unit(g, u):
                lo, hi = UNITS[u]
                pool.wait_ge(s_hi, NU * g + u + 1)
                nc.gpsimd.tensor_tensor(Xlo[:, lo:hi, :], X[:, lo:hi, :], Xhi[:, lo:hi, :].bitcast(F32),
                                        ALU.subtract).then_inc(s_lo[u], 1)

            def full(a, i):
                pool.wait_ge(s_kvm, 2 * a + i + 1)
                nc.gpsimd.tensor_tensor(kvf[i][:], kvm[i][:], kv_cls[:, :HID].unsqueeze(1).broadcast_to([128, HALF_I, HID]),
                                        ALU.add).then_inc(s_kvf, 1)

            def query_sums(a, i):
                pool.wait_ge(s_ks, 2 * a + i + 1)
                pool.wait_ge(s_qts, 2 * a + i + 1)
                nc.gpsimd.tensor_tensor(qs[i][:], qT[i][:], ksum[i][:].unsqueeze(2).broadcast_to([128, HALF_I, SEQ]),
                                        ALU.mult).then_inc(s_qs, 1)

            def group(a, more):
                full(a, 0), full(a, 1)
                query_sums(a, 0), query_sums(a, 1)
                for u in POOL_UNITS if more else ():
                    low_unit(a + 2, u)
                pool.wait_ge(s_rows, 2 * a + 2)
                nc.gpsimd.tensor_copy(logits[:, :, bass.ds(a, 1), :].rearrange("p k s e -> p k (s e)"),
                                      rows[:, :, HID:]).then_inc(s_log, 1)

            for g in two:
                for u in POOL_UNITS:
                    low_unit(g, u)
            pool.wait_ge(s_cv, 5)
            with pool.Fori(0, GROUPS - 2) as a:
                group(a, True)
            group(GROUPS - 2, False)
            group(GROUPS - 1, False)

            def gather(e, i):
                if e >= 2:
                    pool.wait_ge(s_yv, 2 * e - 2)
                for r in range(RT):
                    nc.gpsimd.indirect_dma_start(
                        out=got[i][:, r, :], out_offset=None, in_=rows_dram,
                        in_offset=bass.IndirectOffsetOnAxis(ap=idx[:, e, r:r + 1], axis=0)).then_inc(s_got[i], 16)

            def scatter(e, i):
                pool.wait_ge(s_yv, 2 * e + 2)
                if e > 0:
                    pool.wait_ge(s_add, 16 * RT * e)
                pool.wait_ge(s_ost, 16 * GROUPS)
                for r in range(RT):
                    nc.gpsimd.indirect_dma_start(
                        out=out, out_offset=bass.IndirectOffsetOnAxis(ap=idx[:, e, r:r + 1], axis=0),
                        in_=yv[i][:, r, :], in_offset=None, compute_op=ALU.add).then_inc(s_add, 16)

            pool.wait_ge(s_prob, 16)
            pool.wait_ge(s_ost, 16 * GROUPS)
            pool.wait_ge(s_listp, 1)
            pool.wait_ge(s_idx, 1)
            gather(0, 0)
            for e in range(EXPERTS):
                if e < EXPERTS - 1:
                    gather(e + 1, (e + 1) % 2)
                scatter(e, e % 2)
            pool.wait_ge(s_add, 16 * RT * EXPERTS)


def kernel(x, L0_tok_W, L0_tok_b, L0_tok_class_token, L0_tok_pos_embed, L0_attn_qkv_weight, L0_attn_proj_weight,
           L0_attn_proj_bias, L0_ffn_Wr, L0_ffn_W1, L0_ffn_b1, L0_ffn_W2, L0_ffn_b2):
    import concourse.bacc as bacc
    from concourse.bass_utils import run_bass_kernel_spmd

    def cols(a):
        return np.ascontiguousarray(np.asarray(a).reshape(-1, 1))

    xp = np.asarray(x).reshape(GROUPS, GROUP, CHANNELS, GRID, PATCH, GRID, PATCH).transpose(0, 2, 4, 6, 1, 3, 5)
    xp = xp.reshape(GROUPS, IN_D, GP)
    wt = np.asarray(L0_tok_W).T
    arrays = {
        "xmain": xp[:, :IN_D - TAIL].reshape(GROUPS, CHUNKS - 1, 128, GP).transpose(0, 2, 1, 3),
        "xtail": xp[:, IN_D - TAIL:],
        "wmain": wt[:IN_D - TAIL].reshape(CHUNKS - 1, 128, HID).transpose(1, 0, 2),
        "wtail": wt[IN_D - TAIL:],
        "cst": constants(),
        "tokb": cols(L0_tok_b),
        "cls": cols(L0_tok_class_token),
        "posT": np.asarray(L0_tok_pos_embed).T,
        "wqkvT": np.asarray(L0_attn_qkv_weight).T,
        "projT": np.asarray(L0_attn_proj_weight).T,
        "projb": cols(L0_attn_proj_bias),
        "wr": np.asarray(L0_ffn_Wr),
        "w1": np.asarray(L0_ffn_W1),
        "b1": np.asarray(L0_ffn_b1).reshape(EXPERTS, FT, 128).transpose(0, 2, 1),
        "w2": np.asarray(L0_ffn_W2).reshape(EXPERTS, FT, 128, HID).transpose(0, 2, 1, 3),
        "b2": np.asarray(L0_ffn_b2),
    }
    arrays = {n: np.ascontiguousarray(a) for n, a in arrays.items()}
    nc = bacc.Bacc("TRN2", target_bir_lowering=False, num_devices=1)
    aps = {n: nc.dram_tensor(n, a.shape, F32, kind="ExternalInput").ap() for n, a in arrays.items()}
    aps["out"] = nc.dram_tensor("out", (TOKENS, HID), F32, kind="ExternalOutput").ap()
    tower(nc, **aps)
    r = run_bass_kernel_spmd(nc, [arrays], core_ids=[0])
    return np.asarray(r.results[0]["out"]).reshape(IMAGES, SEQ, HID)
```

```python
from contextlib import ExitStack

import numpy as np

import concourse.bass as bass
from concourse import mybir

F32 = mybir.dt.float32
F32R = mybir.dt.float32r
F16 = mybir.dt.float16
BF16 = mybir.dt.bfloat16
I32 = mybir.dt.int32
ALU = mybir.AluOpType
ACT = mybir.ActivationFunctionType
AX = mybir.AxisListType

IMAGES, CHANNELS, SIDE, PATCH = 128, 3, 224, 28
GRID = SIDE // PATCH
PATCHES = GRID * GRID
SEQ = PATCHES + 1
HID = 128
IN_D = CHANNELS * PATCH * PATCH
HEAD_D = 8
EXPERTS, FFN, CAP = 8, 512, 1024
TOKENS = IMAGES * SEQ

GROUP = 8
GROUPS = IMAGES // GROUP
GP = GROUP * PATCHES
GT = GROUP * SEQ
HALF_I = GROUP // 2
HT = HALF_I * SEQ
CHUNKS = -(-IN_D // 128)
TAIL = IN_D - (CHUNKS - 1) * 128
LOADS = [(0, 6), (6, 12), (12, CHUNKS - 1)]
UNITS = [(0, 3), (3, 6), (6, 9), (9, 12), (12, 15), (15, 17), (17, CHUNKS)]
NU = len(UNITS)
LAST = len(LOADS) - 1
UNITS_OF = [(0, 1), (2, 3), (4, 5, 6)]
POOL_UNITS = (3, 5)
BELOW = slice(64, 64 + TAIL)
TILE = 104
TPG = GT // TILE
TILES = TOKENS // TILE
SEGS = 16
KPS = TILES // SEGS
SEG = TOKENS // SEGS
ROW = HID + EXPERTS
LO, HI = 64, 16
RT = CAP // 128
FT = FFN // 128
PAIRS = EXPERTS // 2
LISTS = [(0, 1), (1, 2), (2, 4), (4, 6), (6, 8)]
LN_EPS, DEN_EPS = 1e-5, 1e-15

C_CENTRE, C_MEAN, C_HEAD, C_IDENT, C_SAME, C_BEFORE, C_ONE = (128 * n for n in range(7))
C_FIRST = C_IDENT + 128
C_PCOL = C_ONE + 128
C_TILE = C_PCOL + 1
C_LO = C_TILE + TILES
C_COLS = C_LO + LO


def constants():
    c = np.zeros((128, C_COLS), np.float32)
    i = np.arange(128)
    c[:, C_CENTRE:C_CENTRE + 128] = np.eye(128) - 1 / 128
    c[:, C_MEAN:C_MEAN + 128] = 1 / 128
    c[:, C_HEAD:C_HEAD + 128] = i[:, None] // HEAD_D == i[None] // HEAD_D
    c[:, C_ONE:C_ONE + 128] = 1
    same = i[:, None] % EXPERTS == i[None] % EXPERTS
    c[:, C_SAME:C_SAME + 128] = same
    c[:, C_BEFORE:C_BEFORE + 128] = same & (i[:, None] // EXPERTS < i[None] // EXPERTS)
    c[:, C_IDENT:C_IDENT + 128] = np.eye(128)
    c[:, C_PCOL] = i
    c[:, C_TILE:C_LO] = np.arange(TILES)
    c[:, C_LO:] = np.arange(LO)
    return c


def tower(nc, xmain, xtail, wmain, wtail, cst, tokb, cls, posT, wqkvT, projT, projb, wr, w1, b1, w2, b2, out):
    rows_dram = nc.dram_tensor("rows_dram", (TOKENS, ROW), F32).ap()
    ctx = ExitStack()
    with ctx:
        def sb(stack, name, shape, dt=F32):
            return stack.enter_context(nc.sbuf_tensor(name, shape, dt))

        def sem(name):
            return ctx.enter_context(nc.semaphore(name))

        C = sb(ctx, "C", [128, C_COLS])
        Wr = sb(ctx, "Wr", [128, EXPERTS])
        logits = sb(ctx, "logits", [TILE, KPS, SEGS, EXPERTS])
        idx = sb(ctx, "idx", [128, EXPERTS, RT], I32)
        centre, mean, heads = (C[:, o:o + 128] for o in (C_CENTRE, C_MEAN, C_HEAD))
        same, before, ones, ident = (C[:, o:o + 128] for o in (C_SAME, C_BEFORE, C_ONE, C_IDENT))
        eps_ln = sb(ctx, "eps_ln", [128, 1])
        eps_den = sb(ctx, "eps_den", [128, 1])

        two = range(2)
        A = ExitStack()
        X = sb(A, "X", [128, CHUNKS, GP])
        Xhi = sb(A, "Xhi", [128, CHUNKS, GP], F32R)
        Xlo = sb(A, "Xlo", [128, CHUNKS - 1, GP], F32R)
        W = sb(A, "W", [128, CHUNKS, HID])
        Whi = sb(A, "Whi", [128, CHUNKS, HID], F32R)
        Wlo = sb(A, "Wlo", [128, CHUNKS, HID], F32R)
        Tokb = sb(A, "Tokb", [128, 1])
        Cls = sb(A, "Cls", [128, 1])
        Pos = sb(A, "Pos", [128, SEQ])
        Wqkv = sb(A, "Wqkv", [128, 3 * HID])
        Proj = sb(A, "Proj", [128, HID])
        Projb = sb(A, "Projb", [128, 1])
        Wc1 = sb(A, "Wc1", [128, 4 * HID])
        Wc1h = sb(A, "Wc1h", [128, 4 * HID], F32R)
        Wc1l = sb(A, "Wc1l", [128, 4 * HID], F32R)
        Wc2 = sb(A, "Wc2", [128, ROW])
        c_col = sb(A, "c_col", [128, 5])
        c_row = sb(A, "c_row", [1, 2 * HID + 1])
        kv_cls = sb(A, "kv_cls", [128, HID + 1])
        hp = sb(A, "hp", [128, GROUP, PATCHES])
        hph = sb(A, "hph", [128, GROUP, PATCHES], F32R)
        hpl = sb(A, "hpl", [128, GROUP, PATCHES], F32R)
        h2 = sb(A, "h2", [128, GROUP, SEQ])
        rows = sb(A, "rows", [TILE, TPG, HID])
        orow = sb(A, "orow", [TILE, TPG, HID])
        sq2 = sb(A, "sq2", [TILE, TPG, HID])
        ss2 = sb(A, "ss2", [TILE, TPG])
        std2 = sb(A, "std2", [TILE, TPG])
        rstd2 = sb(A, "rstd2", [TILE, TPG])
        sq = sb(A, "sq", [128, 4, HID])
        ss = [sb(A, f"ss{i}", [128, 2]) for i in two]
        std = [sb(A, f"std{i}", [128, 2]) for i in two]
        rstd = [sb(A, f"rstd{i}", [128, 2]) for i in two]
        qk = [sb(A, f"qk{i}", [128, 2, 2 * HID]) for i in two]
        vv = [sb(A, f"vv{i}", [128, 2, HID + 1]) for i in two]
        qT = [sb(A, f"qT{i}", [128, HALF_I, SEQ]) for i in two]
        qs = [sb(A, f"qs{i}", [128, HALF_I, SEQ]) for i in two]
        ksum = [sb(A, f"ksum{i}", [128, HALF_I]) for i in two]
        kvm = [sb(A, f"kvm{i}", [128, HALF_I, HID]) for i in two]
        kvf = [sb(A, f"kvf{i}", [128, HALF_I, HID]) for i in two]
        den = [sb(A, f"den{i}", [128, HT]) for i in two]
        rden = [sb(A, f"rden{i}", [128, HT]) for i in two]
        att = [sb(A, f"att{i}", [128, HT]) for i in two]
        A.close()

        B = ExitStack()
        lt = sb(B, "lt", [128, SEG])
        junk = sb(B, "junk", [128, SEG], BF16)
        ge = sb(B, "ge", [128, SEG])
        eq = sb(B, "eq", [128, SEG])
        scan = sb(B, "scan", [128, SEG])
        slot = sb(B, "slot", [128, SEG])
        rmax = sb(B, "rmax", [128, 1])
        mrow = sb(B, "mrow", [1, EXPERTS])
        mb = sb(B, "mb", [TILE, EXPERTS])
        pex = sb(B, "pex", [TILE, KPS * SEGS, EXPERTS])
        psum_e = sb(B, "psum_e", [TILE, EXPERTS])
        prs = sb(B, "prs", [TILE, EXPERTS])
        prob = sb(B, "prob", [TILE, TILES, EXPERTS])
        cnt = sb(B, "cnt", [128, 1], F16)
        cand = sb(B, "cand", [128, 1], I32)
        flip = sb(B, "flip", [128, 1], I32)
        same16 = sb(B, "same16", [128, 128], F16)
        tot = sb(B, "tot", [128, 4])
        room = sb(B, "room", [128, 1])
        sloti = sb(B, "sloti", [TILE, EXPERTS, TILES], I32)
        part_i = sb(B, "part_i", [TILE, 2, EXPERTS * TILES], I32)
        part = sb(B, "part", [TILE, 2, EXPERTS * TILES], BF16)
        tile_b = sb(B, "tile_b", [TILE, TILES], BF16)
        table = sb(B, "table", [TILE, LO, TILES], BF16)
        oh_lo = sb(B, "oh_lo", [TILE, 2, LO, TILES], BF16)
        oh_h = sb(B, "oh_h", [TILE, HI, 2, TILES], BF16)
        oh_hi = [sb(B, f"oh_hi{i}", [TILE, 2, HI, 2, TILES], BF16) for i in two]
        val = sb(B, "val", [128, len(LISTS), 2 * HI])

        W1 = [sb(B, f"W1{i}", [128, FFN]) for i in two]
        B1 = [sb(B, f"B1{i}", [128, FT]) for i in two]
        W2 = [sb(B, f"W2{i}", [128, FT, HID]) for i in two]
        B2 = [sb(B, f"B2{i}", [128, HID]) for i in two]
        got = [sb(B, f"got{i}", [128, RT, ROW]) for i in two]
        W1h = [sb(B, f"W1h{i}", [128, FFN], F32R) for i in two]
        W1l = [sb(B, f"W1l{i}", [128, FFN], F32R) for i in two]
        xeh = [sb(B, f"xeh{i}", [128, CAP], F32R) for i in two]
        xel = [sb(B, f"xel{i}", [128, CAP], F32R) for i in two]
        hid = [sb(B, f"hid{i}", [128, FT, CAP]) for i in two]
        pr = [sb(B, f"pr{i}", [128, RT, 1]) for i in two]
        yb = [sb(B, f"yb{i}", [128, RT, HID]) for i in two]
        yv = [sb(B, f"yv{i}", [128, RT, HID]) for i in two]
        B.close()

        bank = [ctx.enter_context(nc.psum_tensor(f"bank{i}", [128, 512], F32)) for i in range(8)]
        emb = bank[0]
        za, zb, zq = (bank[1], bank[2]), (bank[3], bank[4]), (bank[5], bank[6])

        s_const, s_wraw, s_pad = sem("const_loaded"), [sem(f"embed_weights_loaded{n}") for n in range(len(LOADS))], sem("padding_zero")
        s_wtail, s_const2 = sem("wtail_loaded"), sem("more_constants")
        s_whi, s_wlo = sem("whi_ready"), sem("wlo_ready")
        s_x = [sem(f"x_loaded{n}") for n in range(len(LOADS))]
        s_xt = sem("xtail_loaded")
        s_hi, s_used = sem("xhi_ready"), sem("unit_used")
        s_lo = [sem(f"xlo_ready{u}") for u in range(NU)]
        s_h, s_hh, s_hl = sem("patches_ready"), sem("patches_high"), sem("patches_low")
        s_set, s_ones, s_wc1 = sem("setup_done"), sem("ones_ready"), sem("wc_psum")
        s_cp, s_ca, s_cv = sem("cls_pe"), sem("cls_act"), sem("cls_dve")
        s_z, s_ss, s_std, s_rstd, s_qk, s_vv = (sem(n) for n in ("qkv_psum", "ss1", "std1", "rstd1", "qk_ready", "vv_ready"))
        s_qt, s_qts, s_kv, s_kvm, s_ks, s_kvf, s_qs = (sem(n) for n in (
            "qt_psum", "qt_ready", "kvprod_psum", "kv_masked", "ksum_ready", "kv_full", "qs_ready"))
        s_num, s_den, s_dens, s_rden, s_att = (sem(n) for n in ("num_psum", "den_psum", "den_ready", "rden_ready", "att_ready"))
        s_pr, s_h2 = sem("proj_psum"), sem("h2_ready")
        s_row, s_tr, s_ss2, s_std2, s_rstd2, s_rows, s_orow, s_log = (sem(n) for n in (
            "rows_psum", "otr_psum", "ss2", "std2", "rstd2", "rows_ready", "orow_ready", "logits_kept"))
        s_rst, s_ost = sem("rows_stored"), sem("out_stored")
        s_ltp, s_lt, s_rmax, s_rmaxt, s_mrow, s_mbp, s_mb, s_exp, s_tote, s_prs, s_probr = (
            sem(n) for n in ("lt_psum", "lt_ready", "rowmax", "rowmax_t", "mrow", "max_psum", "max_ready", "exp_ready",
                             "sum_psum", "rsum", "prob_ready"))
        s_cnt, s_tot, s_rej, s_cand = (sem(n) for n in ("counted", "totalled", "rejected", "candidate"))
        s_sel, s_gtot, s_room, s_chosen, s_selt, s_slot, s_slotp = (
            sem(n) for n in ("ties_scanned", "gt_totals", "room", "chosen", "slots_before", "slot_ready", "slot_psum"))
        s_tab, s_part, s_plain, s_ohh, s_ohl, s_listp, s_val, s_idx = (
            sem(n) for n in ("table_ready", "slot_parts", "onehot_hi", "weighted_hi", "onehot_lo", "list_psum", "list_tiles", "idx_ready"))
        s_prob = sem("probs_stored")
        s_wc = [sem(f"expert_loaded{i}") for i in two]
        s_got = [sem(f"gathered{i}") for i in two]
        s_xep, s_xe, s_up, s_hid = sem("xe_psum"), sem("xe_ready"), sem("up_psum"), sem("hid_ready")
        s_xeh, s_w1h, s_w1l = sem("xe_high"), sem("w1_high"), sem("w1_low")
        s_dn, s_yb, s_yv, s_add = sem("down_psum"), sem("yb_ready"), sem("yv_ready"), sem("added")

        block = ctx.enter_context(nc.Block())

        TRIPS = ((0, 3), (3, TPG))

        def first(g):
            return isinstance(g, int) and g == 0

        @block.sync
        def _(sp):
            def load(g, n):
                lo, hi = LOADS[n]
                sp.dma_start(X[:, lo:hi, :], xmain[bass.ds(g, 1), :, lo:hi, :].rearrange("a p c n -> p (a c) n"))\
                    .then_inc(s_x[n], 16)
                if n == len(LOADS) - 1:
                    sp.dma_start(X[:TAIL, CHUNKS - 1, :], xtail[bass.ds(g, 1), :, :].rearrange("a p n -> p (a n)"))\
                        .then_inc(s_xt, 16)

            def reload(g):
                for n in range(len(LOADS)):
                    for u in UNITS_OF[n]:
                        sp.wait_ge(s_lo[u], g)
                    load(g, n)

            def store(a):
                sp.wait_ge(s_rows, 2 * a + 2)
                sp.dma_start(rows_dram.rearrange("(g k p) c -> g p k c", p=TILE, k=TPG)[bass.ds(a, 1), :, :, :HID]
                             .rearrange("g p k c -> (g p) k c"), rows[:]).then_inc(s_rst, 16)
                sp.wait_ge(s_orow, 2 * a + 2)
                sp.dma_start(out.rearrange("(g k p) c -> g p k c", p=TILE, k=TPG)[bass.ds(a, 1), :, :, :]
                             .rearrange("g p k c -> (g p) k c"), orow[:]).then_inc(s_ost, 16)

            for n, (lo, hi) in enumerate(LOADS):
                sp.dma_start(W[:, lo:hi, :], wmain[:, lo:hi, :]).then_inc(s_wraw[n], 16)
                if n < LAST:
                    load(0, n)
            sp.wait_ge(s_pad, 1)
            sp.dma_start(W[:TAIL, CHUNKS - 1, :], wtail).then_inc(s_wtail, 16)
            load(0, LAST)
            for dst, src in ((C[:, :C_FIRST], cst[:, :C_FIRST]), (Wr[:], wr), (Tokb[:], tokb), (Cls[:], cls), (Pos[:], posT),
                             (Wqkv[:], wqkvT), (Proj[:], projT), (Projb[:], projb)):
                sp.dma_start(dst, src).then_inc(s_const, 16)
            reload(1)
            sp.dma_start(C[:, C_FIRST:], cst[:, C_FIRST:]).then_inc(s_const2, 16)
            reload(2)
            with sp.Fori(3, GROUPS) as g:
                reload(g)
                store(g - 3)
            for a in range(GROUPS - 3, GROUPS):
                store(a)

            def weights(e, i):
                sp.dma_start(W1[i][:], w1[bass.ds(e, 1), :, :].rearrange("a p n -> p (a n)")).then_inc(s_wc[i], 16)
                sp.dma_start(B1[i][:], b1[bass.ds(e, 1), :, :].rearrange("a p n -> p (a n)")).then_inc(s_wc[i], 16)
                sp.dma_start(W2[i][:], w2[bass.ds(e, 1), :, :, :].rearrange("a p f n -> p (a f) n")).then_inc(s_wc[i], 16)
                sp.dma_start(B2[i][:], b2[bass.ds(e, 1), :].broadcast_to([128, HID])).then_inc(s_wc[i], 16)

            sp.wait_ge(s_rst, 16 * GROUPS)
            sp.wait_ge(s_ost, 16 * GROUPS)
            sp.wait_ge(s_log, GROUPS)
            weights(0, 0)
            weights(1, 1)

            sp.wait_ge(s_probr, 1)
            sp.dma_start(rows_dram.rearrange("(u p) c -> p u c", p=TILE)[:, :, HID:ROW], prob[:]).then_inc(s_prob, 16)

            with sp.Fori(1, EXPERTS // 2) as j:
                for i in two:
                    sp.wait_ge(s_yv, 4 * j + 2 * i - 2)
                    weights(j * 2 + i, i)

        @block.tensor
        def _(pe):
            def embed(g, lo, hi):
                for c in range(lo, hi):
                    for u, (c0, c1) in enumerate(UNITS):
                        if c == c0:
                            pe.wait_ge(s_lo[u], g + 1)
                    if c == 0 and not first(g):
                        pe.wait_ge(s_h, g)
                    nc.tensor.matmul(emb[:], Whi[:, c, :], Xhi[:, c, :], start=(c == 0), stop=False)
                    if c < CHUNKS - 1:
                        nc.tensor.matmul(emb[:], Whi[:, c, :], Xlo[:, c, :], start=False, stop=False)
                    last = nc.tensor.matmul(emb[:], Wlo[:, c, :], Xhi[:, c, :], start=False, stop=(c == CHUNKS - 1))
                    if any(c + 1 == c1 for _, c1 in UNITS):
                        last.then_inc(s_used, 1)

            def keep_warm(spare, n):
                for _ in range(n):
                    nc.tensor.matmul(spare[:, :256], Whi[:, 0, :], Xhi[:, 0, :256], start=True, stop=True)

            def qkv(a, i):
                pe.wait_ge(s_hl, a + 1)
                if not first(a):
                    pe.wait_ge(s_orow, 2 * a)
                for pair, z in enumerate((za[i], zb[i])):
                    own = slice(HALF_I * i + 2 * pair, HALF_I * i + 2 * pair + 2)
                    high, low = (t[:, own, :].rearrange("p a b -> p (a b)") for t in (hph, hpl))
                    nc.tensor.matmul(z[:], high, Wc1h[:], start=True, stop=False)
                    nc.tensor.matmul(z[:], high, Wc1l[:], start=False, stop=False)
                    nc.tensor.matmul(z[:], low, Wc1h[:], start=False, stop=True).then_inc(s_z, 1)

            def q_columns(a, i):
                pe.wait_ge(s_qk, 4 * a + 2 * i + 2)
                if not first(a):
                    pe.wait_ge(s_rows, 2 * a)
                for pair in two:
                    last = nc.tensor.transpose(zq[i][:, HID * pair:HID * (pair + 1)], qk[i][:, pair, :HID], ident)
                last.then_inc(s_qt, 1)

            def kvprod(a, i):
                pe.wait_ge(s_vv, 4 * a + 2 * i + 2)
                for im in range(HALF_I):
                    r = slice(64 * (im % 2), 64 * (im % 2) + 64)
                    dst = (za, zb)[im % 2][i]
                    last = nc.tensor.matmul(dst[:, 129 * (im // 2):129 * (im // 2) + 129], qk[i][r, im // 2, HID:],
                                            vv[i][r, im // 2, :], start=True, stop=True)
                last.then_inc(s_kv, 1)

            def attend(a, i):
                pe.wait_ge(s_kvf, 2 * a + i + 1)
                pe.wait_ge(s_qts, 2 * a + i + 1)
                for im in range(HALF_I):
                    last = nc.tensor.matmul(zq[i][:, SEQ * im:SEQ * (im + 1)], kvf[i][:, im, :], qT[i][:, im, :],
                                            start=True, stop=True)
                last.then_inc(s_num, 1)
                pe.wait_ge(s_qs, 2 * a + i + 1)
                nc.tensor.matmul(za[i][:, :HT], heads, qs[i][:], start=True, stop=True).then_inc(s_den, 1)

            def project(a, i):
                pe.wait_ge(s_att, 2 * a + i + 1)
                nc.tensor.matmul(zb[i][:, :HT], Proj[:], att[i][:], start=True, stop=True).then_inc(s_pr, 1)

            def to_rows(a):
                pe.wait_ge(s_h2, 4 * a + 4)
                flat = h2[:].rearrange("p a b -> p (a b)")
                for k in range(TPG):
                    last = nc.tensor.matmul(zq[k // 3][:TILE, ROW * (k % 3):ROW * (k % 3 + 1)],
                                            flat[:, TILE * k:TILE * (k + 1)], Wc2[:], start=True, stop=True)
                    if k in (2, TPG - 1):
                        last.then_inc(s_row, 1)
                for k in range(TPG):
                    last = nc.tensor.transpose(za[k // 4][:TILE, HID * (k % 4):HID * (k % 4 + 1)],
                                               flat[:, TILE * k:TILE * (k + 1)], ident)
                    if k in (3, TPG - 1):
                        last.then_inc(s_tr, 1)

            pe.wait_ge(s_wlo, 1)
            embed(0, 0, 6)
            pe.wait_ge(s_wlo, 2)
            embed(0, 6, 12)
            pe.wait_ge(s_set, 1)
            nc.tensor.matmul(za[1][:, :3 * HID], centre, Wqkv[:], start=True, stop=True)
            nc.tensor.matmul(zb[1][:, :EXPERTS], centre, Wr[:], start=True, stop=True).then_inc(s_wc1, 1)
            nc.tensor.matmul(za[0][:, 0:1], centre, c_col[:, 0:1], start=True, stop=True).then_inc(s_cp, 1)
            pe.wait_ge(s_wlo, 4)
            embed(0, 12, 15)
            pe.wait_ge(s_ca, 1)
            nc.tensor.matmul(zb[0][:, 0:1], mean, c_col[:, 1:2], start=True, stop=True).then_inc(s_cp, 1)
            embed(0, 15, 17)
            pe.wait_ge(s_cv, 2)
            nc.tensor.matmul(za[0][0:1, 0:256], c_col[:, 4:5], Wqkv[:, HID:], start=True, stop=True)
            nc.tensor.matmul(zq[0][:, 0:1], Wqkv[:, :HID], c_col[:, 4:5], start=True, stop=True).then_inc(s_cp, 1)
            embed(0, 17, CHUNKS)
            pe.wait_ge(s_ca, 4)
            nc.tensor.matmul(zb[0][:, 0:HID + 1], c_row[:, 0:HID], c_row[:, HID:], start=True, stop=True).then_inc(s_cp, 1)
            keep_warm(zq[1], 16)
            pe.wait_ge(s_cv, 6)

            def both(g, a):
                embed(g, 0, 4)
                qkv(a, 0), qkv(a, 1)
                embed(g, 4, 8)
                q_columns(a, 0), kvprod(a, 0), q_columns(a, 1), kvprod(a, 1)
                embed(g, 8, 11)
                attend(a, 0), attend(a, 1)
                embed(g, 11, 17)
                project(a, 0), project(a, 1)
                embed(g, 17, CHUNKS)
                to_rows(a)

            both(1, 0)
            with pe.Fori(2, GROUPS) as g:
                both(g, g - 1)

            a = GROUPS - 1
            pe.wait_ge(s_h, GROUPS)
            keep_warm(emb, 14)
            qkv(a, 0), qkv(a, 1)
            keep_warm(emb, 5)
            q_columns(a, 0), kvprod(a, 0)
            q_columns(a, 1), kvprod(a, 1)
            keep_warm(emb, 9)
            attend(a, 0)
            attend(a, 1)
            keep_warm(emb, 12)
            project(a, 0)
            keep_warm(emb, 12)
            project(a, 1)
            keep_warm(emb, 6)
            to_rows(a)

            pe.wait_ge(s_log, GROUPS)
            pe.wait_ge(s_orow, 2 * GROUPS)
            for k in range(KPS):
                last = nc.tensor.transpose(bank[k // 4][:, TILE * (k % 4):TILE * (k % 4 + 1)], logits[:, k, :, :].rearrange("p s e -> p (s e)"), ident[:TILE, :TILE])
            last.then_inc(s_ltp, 1)
            def total(n):
                pe.wait_ge(s_cnt, n + 1)
                nc.tensor.matmul(bank[5 + n % 2][:, 0:1], same16[:], cnt[:], start=True, stop=True).then_inc(s_tot, 1)

            pe.wait_ge(s_rows, 2 * GROUPS)
            total(0)
            pe.wait_ge(s_rmax, 1)
            nc.tensor.transpose(bank[2][:1, :128], rmax[:], ident).then_inc(s_rmaxt, 1)
            total(1)
            pe.wait_ge(s_mrow, 1)
            nc.tensor.matmul(bank[3][:TILE, :EXPERTS], ones[:1, :TILE], mrow[:], start=True, stop=True).then_inc(s_mbp, 1)
            for n in range(2, 7):
                total(n)
            pe.wait_ge(s_exp, EXPERTS)
            nc.tensor.matmul(bank[4][:TILE, :EXPERTS], ones[:TILE, :TILE], psum_e[:], start=True, stop=True).then_inc(s_tote, 1)
            for n in range(7, 32):
                total(n)
            pe.wait_ge(s_sel, 1)
            nc.tensor.matmul(bank[5][:, 0:1], same, tot[:, 0:1], start=True, stop=True)
            nc.tensor.matmul(bank[5][:, 1:2], before, tot[:, 1:2], start=True, stop=True).then_inc(s_gtot, 1)
            pe.wait_ge(s_chosen, 1)
            nc.tensor.matmul(bank[6][:, 0:1], before, scan[:, SEG - 1:SEG], start=True, stop=True).then_inc(s_selt, 1)
            pe.wait_ge(s_slot, 1)
            for k in range(KPS):
                last = nc.tensor.transpose(bank[k // 4][:TILE, 128 * (k % 4):128 * (k % 4 + 1)],
                                           slot[:, TILE * k:TILE * (k + 1)], ident)
            last.then_inc(s_slotp, 1)

            def make_list(n, bank_l):
                w = LISTS[n][1] - LISTS[n][0]
                pe.wait_ge(s_ohh, n + 1)
                pe.wait_ge(s_ohl, n + 1)
                for u in range(TILES):
                    last = nc.tensor.matmul(bank_l[:LO * w, :2 * HI * w], oh_lo[:, :w, :, u].rearrange("p e a -> p (e a)"),
                                            oh_hi[n % 2][:, :, :, :w, u].rearrange("p v a e -> p v e a"),
                                            start=(u == 0), stop=(u == TILES - 1))
                last.then_inc(s_listp, 1)

            def columns(j, i):
                n = 2 * j + i
                pe.wait_ge(s_got[i], 16 * RT * (j + 1))
                if not (first(j) and i == 0):
                    pe.wait_ge(s_xe, 2 * n)
                for r in range(RT):
                    last = nc.tensor.transpose(bank[r // 4][:, 128 * (r % 4):128 * (r % 4 + 1)], got[i][:, r, :HID], ident)
                    if r % 4 == 3:
                        last.then_inc(s_xep, 1)

            def up(j, i):
                n = 2 * j + i
                pe.wait_ge(s_w1l, n + 1)
                for half in two:
                    pe.wait_ge(s_xe, 2 * n + half + 1)
                    for f in range(FT):
                        m = FT * half + f
                        if not (first(j) and i == 0 and m < 4):
                            pe.wait_ge(s_hid, 8 * n + m - 3)
                        high, low = (t[i][:, 128 * f:128 * (f + 1)] for t in (W1h, W1l))
                        xhigh, xlow = (t[i][:, 512 * half:512 * (half + 1)] for t in (xeh, xel))
                        nc.tensor.matmul(bank[2 + m % 4][:], high, xhigh, start=True, stop=False)
                        nc.tensor.matmul(bank[2 + m % 4][:], high, xlow, start=False, stop=False)
                        nc.tensor.matmul(bank[2 + m % 4][:], low, xhigh, start=False, stop=True).then_inc(s_up, 1)

            def down(j, i):
                n = 2 * j + i
                for half in two:
                    pe.wait_ge(s_hid, 8 * n + 4 * half + 4)
                    if not (first(j) and i == 0):
                        pe.wait_ge(s_yb, 2 * n + half - 1)
                    for r in range(4):
                        t = 4 * half + r
                        for f in range(FT):
                            last = nc.tensor.matmul(bank[6 + half][:, 128 * r:128 * (r + 1)],
                                                    hid[i][:, f, 128 * t:128 * (t + 1)], W2[i][:, f, :],
                                                    start=(f == 0 and r == 0), stop=(f == FT - 1), skip_group_check=True)
                    last.then_inc(s_dn, 1)

            def keep_warm_b(n):
                for _ in range(n):
                    nc.tensor.matmul(bank[2][:, :128], same16[:], same16[:], start=True, stop=True)

            keep_warm_b(64)
            make_list(0, bank[7])
            keep_warm_b(80)
            make_list(1, bank[7])
            keep_warm_b(56)
            columns(0, 0)
            keep_warm_b(40)
            make_list(2, bank[7])
            up(0, 0)
            columns(0, 1)
            pe.wait_ge(s_idx, 3)
            down(0, 0)
            pe.wait_ge(s_xe, 4)
            make_list(3, bank[0])
            up(0, 1)
            pe.wait_ge(s_idx, 4)
            columns(1, 0), down(0, 1)
            pe.wait_ge(s_xe, 6)
            make_list(4, bank[0])
            pe.wait_ge(s_idx, 5)
            with pe.Fori(1, PAIRS - 1) as j:
                up(j, 0), columns(j, 1), down(j, 0)
                up(j, 1), columns(j + 1, 0), down(j, 1)
            up(PAIRS - 1, 0), columns(PAIRS - 1, 1), down(PAIRS - 1, 0)
            up(PAIRS - 1, 1), down(PAIRS - 1, 1)

        @block.scalar
        def _(act):
            def round_unit(g, u):
                lo, hi = UNITS[u]
                for n, (a, b) in enumerate(LOADS):
                    if lo == a:
                        act.wait_ge(s_x[n], 16 * g + 16)
                if hi == CHUNKS:
                    act.wait_ge(s_xt, 16 * g + 16)
                if not first(g):
                    act.wait_ge(s_used, NU * (g - 1) + u + 1)
                nc.scalar.activation(Xhi[:, lo:hi, :], X[:, lo:hi, :], ACT.Copy).then_inc(s_hi, 1)

            def round_patches(g):
                act.wait_ge(s_h, g + 1)
                nc.scalar.activation(hph[:], hp[:], ACT.Copy).then_inc(s_hh, 1)

            def squares(a, i):
                for pair, z in enumerate((za[i], zb[i])):
                    act.wait_ge(s_z, 4 * a + 2 * i + pair + 1)
                    nc.scalar.activation(sq[:, 2 * i + pair], z[:, :HID], ACT.Square, accum_out=ss[i][:, pair:pair + 1]).then_inc(s_ss, 1)
                act.wait_ge(s_ss, 4 * a + 2 * i + 2)
                nc.scalar.activation(std[i][:], ss[i][:], ACT.Sqrt, bias=eps_ln[:], scale=1 / HID).then_inc(s_std, 1)

            def values(a, i):
                for pair, z in enumerate((za[i], zb[i])):
                    act.wait_ge(s_qk, 4 * a + 2 * i + pair + 1)
                    nc.scalar.activation(vv[i][:, pair, :HID], z[:, 3 * HID:], ACT.Copy,
                                         scale=rstd[i][:, pair:pair + 1]).then_inc(s_vv, 1)

            def q_columns(a, i):
                act.wait_ge(s_qt, 2 * a + i + 1)
                nc.scalar.activation(qT[i][:, :, 1:], zq[i][:, :2 * HID].rearrange("p (a b) -> p a b", b=PATCHES),
                                     ACT.Copy).then_inc(s_qts, 1)

            def denominator(a, i):
                act.wait_ge(s_den, 2 * a + i + 1)
                nc.scalar.activation(den[i][:], za[i][:, :HT], ACT.Identity, bias=eps_den[:]).then_inc(s_dens, 1)

            def row_squares(a):
                for n, (lo, hi) in enumerate(TRIPS):
                    act.wait_ge(s_row, 2 * a + n + 1)
                    for k in range(lo, hi):
                        nc.scalar.activation(sq2[:, k], zq[n][:TILE, ROW * (k - lo):ROW * (k - lo) + HID], ACT.Square,
                                             accum_out=ss2[:, k:k + 1]).then_inc(s_ss2, 1)
                act.wait_ge(s_ss2, TPG * a + TPG)
                nc.scalar.activation(std2[:], ss2[:], ACT.Sqrt, bias=eps_ln[:TILE], scale=1 / HID).then_inc(s_std2, 1)

            def to_rows(a):
                for n, (lo, hi) in enumerate(((0, 4), (4, TPG))):
                    act.wait_ge(s_tr, 2 * a + n + 1)
                    if n == 0 and not first(a):
                        act.wait_ge(s_ost, 16 * a)
                    nc.scalar.activation(orow[:, lo:hi, :], za[n][:TILE, :HID * (hi - lo)].rearrange("p (k c) -> p k c", c=HID),
                                         ACT.Copy).then_inc(s_orow, 1)
                act.wait_ge(s_log, a + 1)
                if not first(a):
                    act.wait_ge(s_rst, 16 * a)
                for n, (lo, hi) in enumerate(TRIPS):
                    for k in range(lo, hi):
                        last = nc.scalar.activation(rows[:, k, :], zq[n][:TILE, ROW * (k - lo):ROW * (k - lo) + HID], ACT.Copy,
                                                    scale=rstd2[:, k:k + 1])
                    last.then_inc(s_rows, 1)

            def group(a, more, embedding):
                def rounding(*units):
                    for u in units if more else ():
                        round_unit(a + 2, u)

                squares(a, 0), squares(a, 1)
                values(a, 0), values(a, 1)
                q_columns(a, 0), q_columns(a, 1)
                rounding(0, 1, 2)
                denominator(a, 0), denominator(a, 1)
                rounding(3, 4, 5, 6)
                if embedding:
                    round_patches(a + 1)
                row_squares(a)
                to_rows(a)

            def round_weights(n):
                lo, hi = LOADS[n][0], CHUNKS if n == LAST else LOADS[n][1]
                act.wait_ge(s_wraw[n], 16)
                if n == LAST:
                    act.wait_ge(s_wtail, 16)
                nc.scalar.activation(Whi[:, lo:hi, :], W[:, lo:hi, :], ACT.Copy).then_inc(s_whi, 1)

            for n in range(LAST):
                round_weights(n)
                for u in UNITS_OF[n]:
                    round_unit(0, u)
            round_weights(LAST)
            for u in UNITS_OF[LAST]:
                round_unit(0, u)

            act.wait_ge(s_ones, 1)
            act.wait_ge(s_cp, 1)
            nc.scalar.activation(c_col[:, 1:2], za[0][:, 0:1], ACT.Square).then_inc(s_ca, 1)
            act.wait_ge(s_cp, 2)
            nc.scalar.activation(c_col[:, 2:3], zb[0][:, 0:1], ACT.Sqrt, bias=eps_ln[:]).then_inc(s_ca, 1)
            round_unit(1, 0)
            act.wait_ge(s_cp, 3)
            nc.scalar.activation(c_row[:, :HID], za[0][:1, :HID], ACT.Relu).then_inc(s_ca, 1)
            nc.scalar.activation(c_row[:, HID:2 * HID], za[0][:1, HID:256], ACT.Copy).then_inc(s_ca, 1)

            act.wait_ge(s_cv, 3)
            nc.scalar.activation(Wc1h[:], Wc1[:], ACT.Copy).then_inc(s_ca, 1)

            round_patches(0)
            round_unit(1, 1), round_unit(1, 2), round_unit(1, 3)
            squares(0, 0), squares(0, 1)
            values(0, 0), values(0, 1)
            round_unit(1, 4)
            q_columns(0, 0), q_columns(0, 1)
            round_unit(1, 5), round_unit(1, 6), round_unit(2, 0)
            denominator(0, 0), denominator(0, 1)
            for u in range(1, 5):
                round_unit(2, u)
            round_patches(1)
            row_squares(0)
            to_rows(0)
            round_unit(2, 5), round_unit(2, 6)
            with act.Fori(1, GROUPS - 2) as a:
                group(a, True, True)
            group(GROUPS - 2, False, True)
            group(GROUPS - 1, False, False)

            act.wait_ge(s_mb, 1)
            for e in range(EXPERTS):
                nc.scalar.activation(pex[:, :, e], logits[:, :, :, e].rearrange("p k s -> p (k s)"), ACT.Exp,
                                     bias=mb[:, e:e + 1], accum_out=psum_e[:, e:e + 1]).then_inc(s_exp, 1)
            nc.scalar.activation(tile_b[:], C[:TILE, C_TILE:C_LO], ACT.Copy)
            nc.scalar.activation(table[:], C[:TILE, C_LO:].unsqueeze(2).broadcast_to([TILE, LO, TILES]), ACT.Copy).then_inc(s_tab, 1)
            act.wait_ge(s_prs, 1)
            act.wait_ge(s_exp, EXPERTS)
            for e in range(EXPERTS):
                last = nc.scalar.activation(prob[:, :, e].rearrange("p (s k) -> p k s", k=KPS),
                                            pex[:, :, e].rearrange("p (k s) -> p k s", k=KPS), ACT.Copy, scale=prs[:, e:e + 1])
            last.then_inc(s_probr, 1)

            def highs(j, i):
                n = 2 * j + i
                act.wait_ge(s_wc[i], 64 * (j + 1))
                nc.scalar.activation(W1h[i][:], W1[i][:], ACT.Copy).then_inc(s_w1h, 1)
                for half in two:
                    act.wait_ge(s_xep, 2 * n + half + 1)
                    nc.scalar.activation(xeh[i][:, 512 * half:512 * (half + 1)], bank[half][:], ACT.Copy).then_inc(s_xeh, 1)

            def hidden(j, i):
                n = 2 * j + i
                for m in range(2 * FT):
                    half, f = m // FT, m % FT
                    act.wait_ge(s_up, 8 * n + m + 1)
                    if m == 0 and not first(j):
                        act.wait_ge(s_dn, 2 * n - 2)
                    nc.scalar.activation(hid[i][:, f, 512 * half:512 * (half + 1)], bank[2 + m % 4][:], ACT.Gelu,
                                         bias=B1[i][:, f:f + 1]).then_inc(s_hid, 1)

            highs(0, 0), hidden(0, 0)
            highs(0, 1), hidden(0, 1)
            with act.Fori(1, EXPERTS // 2) as j:
                highs(j, 0), hidden(j, 0)
                highs(j, 1), hidden(j, 1)

        @block.vector
        def _(dve):
            def low_unit(g, u):
                lo, hi = UNITS[u]
                dve.wait_ge(s_hi, NU * g + u + 1)
                if u == NU - 1:
                    hi = CHUNKS - 1
                    nc.vector.tensor_tensor(Xhi[BELOW, hi, :], X[:TAIL, hi, :], Xhi[:TAIL, hi, :].bitcast(F32), ALU.subtract)
                nc.vector.tensor_tensor(Xlo[:, lo:hi, :], X[:, lo:hi, :], Xhi[:, lo:hi, :].bitcast(F32),
                                        ALU.subtract).then_inc(s_lo[u], 1)

            def evacuate(g):
                if not first(g):
                    dve.wait_ge(s_h2, 4 * g)
                dve.wait_ge(s_used, NU * g + NU)
                nc.vector.scalar_tensor_tensor(
                    out=hp[:], in0=emb[:].rearrange("p (b n) -> p b n", b=GROUP), scalar=Tokb[:],
                    in1=Pos[:, 1:].unsqueeze(1).broadcast_to([128, GROUP, PATCHES]), op0=ALU.add, op1=ALU.mult).then_inc(s_h, 1)

            def low_patches(g):
                dve.wait_ge(s_hh, g + 1)
                nc.vector.tensor_tensor(hpl[:], hp[:], hph[:].bitcast(F32), ALU.subtract).then_inc(s_hl, 1)

            def norm_qk(a, i):
                dve.wait_ge(s_std, 2 * a + i + 1)
                nc.vector.reciprocal(rstd[i][:], std[i][:]).then_inc(s_rstd, 1)
                dve.wait_ge(s_rstd, 2 * a + i + 1)
                for pair, z in enumerate((za[i], zb[i])):
                    nc.vector.tensor_scalar(qk[i][:, pair, :], z[:, HID:3 * HID], rstd[i][:, pair:pair + 1], 0.0,
                                            ALU.mult, ALU.max).then_inc(s_qk, 1)

            def mask(a, i):
                dve.wait_ge(s_kv, 2 * a + i + 1)
                for n, z in enumerate((za, zb)):
                    kv = z[i][:, :258].rearrange("p (b c) -> p b c", b=2)
                    last = nc.vector.tensor_tensor(kvm[i][:, n::2, :], kv[:, :, :HID],
                                                   heads.unsqueeze(1).broadcast_to([128, 2, HID]), ALU.mult)
                last.then_inc(s_kvm, 1)
                for n, z in enumerate((za, zb)):
                    kv = z[i][:, :258].rearrange("p (b c) -> p b c", b=2)
                    last = nc.vector.tensor_scalar(ksum[i][:, n::2].unsqueeze(2), kv[:, :, HID:], kv_cls[:, HID:], None, ALU.add)
                last.then_inc(s_ks, 1)

            def attention(a, i):
                dve.wait_ge(s_dens, 2 * a + i + 1)
                nc.vector.reciprocal(rden[i][:], den[i][:]).then_inc(s_rden, 1)
                dve.wait_ge(s_rden, 2 * a + i + 1)
                dve.wait_ge(s_num, 2 * a + i + 1)
                nc.vector.tensor_tensor(att[i][:], zq[i][:, :HT], rden[i][:], ALU.mult).then_inc(s_att, 1)

            def residual(a, i):
                dve.wait_ge(s_pr, 2 * a + i + 1)
                own = slice(HALF_I * i, HALF_I * (i + 1))
                pr = zb[i][:, :HT].rearrange("p (a b) -> p a b", b=SEQ)
                nc.vector.scalar_tensor_tensor(out=h2[:, own, 1:], in0=pr[:, :, 1:], scalar=Projb[:], in1=hp[:, own, :],
                                               op0=ALU.add, op1=ALU.add).then_inc(s_h2, 1)
                nc.vector.scalar_tensor_tensor(out=h2[:, own, 0], in0=pr[:, :, 0], scalar=Projb[:],
                                               in1=c_col[:, 0:1].broadcast_to([128, HALF_I]),
                                               op0=ALU.add, op1=ALU.add).then_inc(s_h2, 1)

            def norm_rows(a):
                dve.wait_ge(s_std2, a + 1)
                nc.vector.reciprocal(rstd2[:], std2[:]).then_inc(s_rstd2, 1)
                dve.wait_ge(s_rstd2, a + 1)
                for n, (lo, hi) in enumerate(TRIPS):
                    last = nc.vector.tensor_tensor(
                        logits[:, lo:hi, bass.ds(a, 1), :].rearrange("p k s e -> p k (s e)"),
                        zq[n][:TILE, :ROW * (hi - lo)].rearrange("p (k c) -> p k c", c=ROW)[:, :, HID:],
                        rstd2[:, lo:hi].unsqueeze(2).broadcast_to([TILE, hi - lo, EXPERTS]), ALU.mult)
                last.then_inc(s_log, 1)

            def group(a, more, embedding):
                def low(*units):
                    for u in units if more else ():
                        low_unit(a + 2, u)

                norm_qk(a, 0), norm_qk(a, 1)
                mask(a, 0), mask(a, 1)
                low(0, 1)
                attention(a, 0), attention(a, 1)
                residual(a, 0), residual(a, 1)
                if embedding:
                    evacuate(a + 1)
                    low_patches(a + 1)
                low(2)
                norm_rows(a)
                low(4, 6)

            nc.vector.memset(W[:, CHUNKS - 1, :], 0.0)
            nc.vector.memset(X[:, CHUNKS - 1, :], 0.0).then_inc(s_pad, 1)
            nc.vector.memset(eps_ln[:], LN_EPS)
            nc.vector.memset(eps_den[:], DEN_EPS)
            nc.vector.memset(c_row[:, 2 * HID:], 1.0)
            for i in two:
                last = nc.vector.memset(vv[i][:, :, HID:], 1.0)
            last.then_inc(s_ones, 1)

            def low_weights(n):
                lo, hi = LOADS[n][0], CHUNKS if n == LAST else LOADS[n][1]
                dve.wait_ge(s_whi, n + 1)
                nc.vector.tensor_tensor(Wlo[:, lo:hi, :], W[:, lo:hi, :], Whi[:, lo:hi, :].bitcast(F32),
                                        ALU.subtract).then_inc(s_wlo, 1)

            for n in range(LAST):
                low_weights(n)
                for u in UNITS_OF[n]:
                    low_unit(0, u)
            low_weights(LAST)
            dve.wait_ge(s_wlo, LAST + 1)
            nc.vector.tensor_copy(Whi[BELOW, CHUNKS - 1, :], W[:TAIL, CHUNKS - 1, :]).then_inc(s_wlo, 1)

            dve.wait_ge(s_const, 16 * 8)
            nc.vector.tensor_tensor(c_col[:, 0:1], Cls[:], Pos[:, 0:1], ALU.mult).then_inc(s_set, 1)
            for u in UNITS_OF[LAST]:
                if u not in POOL_UNITS:
                    low_unit(0, u)
            dve.wait_ge(s_ca, 2)
            nc.vector.reciprocal(c_col[:, 3:4], c_col[:, 2:3]).then_inc(s_cv, 1)
            dve.wait_ge(s_cv, 1)
            nc.vector.tensor_tensor(c_col[:, 4:5], za[0][:, 0:1], c_col[:, 3:4], ALU.mult).then_inc(s_cv, 1)
            dve.wait_ge(s_wc1, 1)
            for w in (Wc1, Wc2):
                nc.vector.tensor_copy(w[:, :HID], centre)
            nc.vector.tensor_copy(Wc1[:, HID:], za[1][:, :3 * HID])
            nc.vector.tensor_copy(Wc2[:, HID:], zb[1][:, :EXPERTS]).then_inc(s_cv, 1)
            low_unit(1, 0)
            dve.wait_ge(s_cp, 4)
            nc.vector.tensor_tensor(kv_cls[:, :HID], zb[0][:, :HID], heads, ALU.mult)
            nc.vector.tensor_copy(kv_cls[:, HID:], zb[0][:, HID:HID + 1]).then_inc(s_cv, 1)
            for i in two:
                last = nc.vector.tensor_scalar(qT[i][:, :, 0], zq[0][:, 0:1].broadcast_to([128, HALF_I]), 0.0, None, ALU.max)
            last.then_inc(s_cv, 1)
            evacuate(0)
            dve.wait_ge(s_ca, 5)
            nc.vector.tensor_tensor(Wc1l[:], Wc1[:], Wc1h[:].bitcast(F32), ALU.subtract).then_inc(s_cv, 1)
            low_patches(0)
            dve.wait_ge(s_cv, 6)

            low_unit(1, 1), low_unit(1, 2)
            norm_qk(0, 0), norm_qk(0, 1)
            low_unit(1, 4)
            mask(0, 0), mask(0, 1)
            low_unit(1, 5), low_unit(1, 6), low_unit(2, 0)
            attention(0, 0), attention(0, 1)
            low_unit(2, 1)
            residual(0, 0), residual(0, 1)
            evacuate(1)
            low_unit(2, 2)
            low_patches(1)
            norm_rows(0)
            low_unit(2, 4), low_unit(2, 6)
            with dve.Fori(1, GROUPS - 2) as a:
                group(a, True, True)
            group(GROUPS - 2, False, True)
            group(GROUPS - 1, False, False)

            dve.wait_ge(s_const2, 16)
            nc.vector.tensor_copy(same16[:], same)
            dve.wait_ge(s_ltp, 1)
            nc.vector.tensor_copy(lt[:, :4 * TILE], bank[0][:, :4 * TILE])
            nc.vector.tensor_copy(lt[:, 4 * TILE:], bank[1][:, :TILE]).then_inc(s_lt, 1)
            dve.wait_ge(s_lt, 1)

            def count(n, threshold):
                nc.vector.tensor_scalar(junk[:], lt[:], threshold, None, ALU.is_ge, ALU.add, accum_out=cnt[:]).then_inc(s_cnt, 1)

            BIT = [1 << (30 - n) for n in range(31)]
            count(0, 0.0)
            nc.vector.reduce_max(rmax[:], lt[:], axis=AX.X).then_inc(s_rmax, 1)
            dve.wait_ge(s_tot, 1)
            nc.vector.tensor_scalar(flip[:], bank[5][:, 0:1], float(CAP), -1.0, ALU.is_lt, ALU.mult).then_inc(s_rej, 1)
            dve.wait_ge(s_rej, 1)
            nc.vector.tensor_scalar(cand[:], flip[:], BIT[0], None, ALU.bitwise_xor).then_inc(s_cand, 1)
            for n in range(1, 32):
                dve.wait_ge(s_cand, n)
                count(n, cand[:].bitcast(F32))
                if n == 1:
                    dve.wait_ge(s_rmaxt, 1)
                    nc.vector.reduce_max(mrow[:], bank[2][:1, :128].rearrange("p (s e) -> p e s", e=EXPERTS), axis=AX.X).then_inc(s_mrow, 1)
                if n == 2:
                    dve.wait_ge(s_mbp, 1)
                    nc.vector.tensor_scalar(mb[:], bank[3][:TILE, :EXPERTS], -1.0, None, ALU.mult).then_inc(s_mb, 1)
                if n == 7:
                    dve.wait_ge(s_tote, 1)
                    nc.vector.reciprocal(prs[:], bank[4][:TILE, :EXPERTS]).then_inc(s_prs, 1)
                dve.wait_ge(s_tot, n + 1)
                nc.vector.tensor_scalar(flip[:], bank[5 + n % 2][:, 0:1], float(CAP), float(BIT[n - 1]), ALU.is_lt, ALU.mult)\
                    .then_inc(s_rej, 1)
                dve.wait_ge(s_rej, n + 1)
                if n < 31:
                    nc.vector.scalar_tensor_tensor(out=cand[:], in0=cand[:], scalar=BIT[n], in1=flip[:],
                                                   op0=ALU.bitwise_xor, op1=ALU.bitwise_xor).then_inc(s_cand, 1)
                else:
                    nc.vector.tensor_tensor(cand[:], cand[:], flip[:], ALU.bitwise_xor).then_inc(s_cand, 1)
            dve.wait_ge(s_cand, 32)

            T = cand[:].bitcast(F32)
            nc.vector.tensor_scalar(ge[:], lt[:], T, None, ALU.is_gt, ALU.add, accum_out=tot[:, 0:1])
            nc.vector.tensor_scalar(eq[:], lt[:], T, None, ALU.is_equal, ALU.add, accum_out=tot[:, 1:2]).then_inc(s_sel, 1)
            dve.wait_ge(s_sel, 1)
            nc.vector.tensor_tensor_scan(scan[:], eq[:], eq[:], 0.0, ALU.add, ALU.max).then_inc(s_sel, 1)
            dve.wait_ge(s_gtot, 1)
            nc.vector.tensor_scalar(tot[:, 2:3], bank[5][:, 0:1], -1.0, float(CAP), ALU.mult, ALU.add).then_inc(s_sel, 1)
            dve.wait_ge(s_sel, 3)
            nc.vector.tensor_tensor(room[:], tot[:, 2:3], bank[5][:, 1:2], ALU.subtract).then_inc(s_room, 1)
            dve.wait_ge(s_room, 1)
            nc.vector.scalar_tensor_tensor(out=eq[:], in0=scan[:], scalar=room[:], in1=eq[:],
                                           op0=ALU.is_le, op1=ALU.mult).then_inc(s_room, 1)
            dve.wait_ge(s_room, 2)
            nc.vector.tensor_tensor(ge[:], ge[:], eq[:], ALU.add).then_inc(s_room, 1)
            dve.wait_ge(s_room, 3)
            nc.vector.tensor_tensor_scan(scan[:], ge[:], ge[:], 0.0, ALU.add, ALU.max).then_inc(s_chosen, 1)
            dve.wait_ge(s_chosen, 1)
            dve.wait_ge(s_selt, 1)
            nc.vector.tensor_copy(room[:], bank[6][:, 0:1]).then_inc(s_room, 1)
            dve.wait_ge(s_room, 4)
            nc.vector.scalar_tensor_tensor(out=slot[:], in0=scan[:], scalar=room[:], in1=ge[:],
                                           op0=ALU.add, op1=ALU.mult).then_inc(s_slot, 1)
            dve.wait_ge(s_slotp, 1)

            def parts(lo, hi, done):
                for n, (k0, k1) in enumerate(((0, 4), (4, KPS))):
                    last = nc.vector.tensor_scalar(
                        sloti[:].rearrange("p e (s k) -> p k s e", k=KPS)[:, k0:k1, :, lo:hi],
                        bank[n][:TILE, :128 * (k1 - k0)].rearrange("p (k s e) -> p k s e", s=SEGS, e=EXPERTS)[:, :, :, lo:hi],
                        -1.0, None, ALU.add)
                last.then_inc(s_part, 1)
                dve.wait_ge(s_part, done + 1)
                own = slice(TILES * lo, TILES * hi)
                slots = sloti[:].rearrange("p e u -> p (e u)")[:, own]
                nc.vector.tensor_scalar(part_i[:, 0, own], slots, LO - 1, None, ALU.bitwise_and)
                nc.vector.tensor_scalar(part_i[:, 1, own], slots, LO.bit_length() - 1, None, ALU.arith_shift_right).then_inc(s_part, 1)
                dve.wait_ge(s_part, done + 2)
                nc.vector.tensor_copy(part[:, :, own], part_i[:, :, own]).then_inc(s_part, 1)
                dve.wait_ge(s_part, done + 3)

            def own(which, n):
                lo, hi = LISTS[n]
                return part[:, which, TILES * lo:TILES * hi].rearrange("p (e u) -> p e u", e=hi - lo)

            def high(n):
                dst, w = oh_hi[n % 2], LISTS[n][1] - LISTS[n][0]
                if n >= 1:
                    dve.wait_ge(s_ohh, n)
                if n >= 2:
                    dve.wait_ge(s_listp, n - 1)
                nc.vector.tensor_tensor(oh_h[:, :, :w], own(1, n).unsqueeze(1).broadcast_to([TILE, HI, w, TILES]),
                                        table[:, :HI].unsqueeze(2).broadcast_to([TILE, HI, w, TILES]), ALU.is_equal).then_inc(s_plain, 1)
                dve.wait_ge(s_plain, n + 1)
                nc.vector.tensor_scalar(dst[:, 0, :, :w], oh_h[:, :, :w], C[:TILE, C_PCOL:C_PCOL + 1], None, ALU.mult)
                nc.vector.tensor_tensor(dst[:, 1, :, :w], oh_h[:, :, :w],
                                        tile_b[:].unsqueeze(1).unsqueeze(1).broadcast_to([TILE, HI, w, TILES]), ALU.mult).then_inc(s_ohh, 1)

            def low_part(n):
                w = LISTS[n][1] - LISTS[n][0]
                if n >= 1:
                    dve.wait_ge(s_listp, n)
                nc.vector.tensor_tensor(oh_lo[:, :w], own(0, n).unsqueeze(2).broadcast_to([TILE, w, LO, TILES]),
                                        table[:].unsqueeze(1).broadcast_to([TILE, w, LO, TILES]), ALU.is_equal).then_inc(s_ohl, 1)

            def indices(n, bank_l):
                first_e, w = LISTS[n][0], LISTS[n][1] - LISTS[n][0]
                dve.wait_ge(s_listp, n + 1)
                nc.vector.tensor_copy(val[:LO * w, n, :HI * w], bank_l[:LO * w, HI * w:2 * HI * w]).then_inc(s_val, 1)
                dve.wait_ge(s_val, n + 1)
                for e in range(w):
                    for h in two:
                        p_, u_ = (t[LO * e:LO * (e + 1), HI * e:HI * (e + 1)].rearrange("p (r h) -> p r h", h=2)[:, :, h]
                                  for t in (bank_l, val[:, n, :]))
                        last = nc.vector.scalar_tensor_tensor(out=idx[LO * h:LO * (h + 1), first_e + e, :], in0=u_,
                                                              scalar=float(TILE), in1=p_, op0=ALU.mult, op1=ALU.add)
                last.then_inc(s_idx, 1)

            def inputs(j, i):
                n = 2 * j + i
                if not first(j):
                    dve.wait_ge(s_yv, 2 * n - 2)
                dve.wait_ge(s_w1h, n + 1)
                nc.vector.tensor_tensor(W1l[i][:], W1[i][:], W1h[i][:].bitcast(F32), ALU.subtract).then_inc(s_w1l, 1)
                for half in two:
                    own = slice(512 * half, 512 * (half + 1))
                    dve.wait_ge(s_xeh, 2 * n + half + 1)
                    if half == 0:
                        e = HID + n
                        nc.vector.tensor_copy(pr[i][:], got[i][:, :, bass.ds(e, 1)])
                    nc.vector.tensor_tensor(xel[i][:, own], bank[half][:], xeh[i][:, own].bitcast(F32), ALU.subtract).then_inc(s_xe, 1)

            def outputs(j, i):
                n = 2 * j + i
                for half in two:
                    dve.wait_ge(s_dn, 2 * n + half + 1)
                    dve.wait_ge(s_wc[i], 64 * (j + 1))
                    r = slice(4 * half, 4 * half + 4)
                    nc.vector.tensor_tensor(yb[i][:, r, :], bank[6 + half][:].rearrange("p (r c) -> p r c", c=HID),
                                            B2[i][:].unsqueeze(1).broadcast_to([128, 4, HID]), ALU.add).then_inc(s_yb, 1)
                    dve.wait_ge(s_yb, 2 * n + half + 1)
                    if not first(j):
                        dve.wait_ge(s_add, 16 * RT * (n - 1))
                    nc.vector.tensor_tensor(yv[i][:, r, :], yb[i][:, r, :],
                                            pr[i][:, r, :].broadcast_to([128, 4, HID]), ALU.mult).then_inc(s_yv, 1)

            parts(0, 1, 0)
            dve.wait_ge(s_tab, 1)
            high(0), low_part(0)
            parts(1, EXPERTS, 3)
            indices(0, bank[7]), high(1)
            low_part(1), high(2), indices(1, bank[7])
            low_part(2)
            inputs(0, 0)
            indices(2, bank[7])
            high(3)
            inputs(0, 1)
            low_part(3)
            outputs(0, 0)
            indices(3, bank[0])
            high(4)
            inputs(1, 0)
            low_part(4)
            outputs(0, 1)
            indices(4, bank[0])
            with dve.Fori(1, PAIRS - 1) as j:
                inputs(j, 1), outputs(j, 0)
                inputs(j + 1, 0), outputs(j, 1)
            inputs(PAIRS - 1, 1), outputs(PAIRS - 1, 0)
            outputs(PAIRS - 1, 1)

        @block.gpsimd
        def _(pool):
            def low_unit(g, u):
                lo, hi = UNITS[u]
                pool.wait_ge(s_hi, NU * g + u + 1)
                nc.gpsimd.tensor_tensor(Xlo[:, lo:hi, :], X[:, lo:hi, :], Xhi[:, lo:hi, :].bitcast(F32),
                                        ALU.subtract).then_inc(s_lo[u], 1)

            def full(a, i):
                pool.wait_ge(s_kvm, 2 * a + i + 1)
                nc.gpsimd.tensor_tensor(kvf[i][:], kvm[i][:], kv_cls[:, :HID].unsqueeze(1).broadcast_to([128, HALF_I, HID]),
                                        ALU.add).then_inc(s_kvf, 1)

            def query_sums(a, i):
                pool.wait_ge(s_ks, 2 * a + i + 1)
                pool.wait_ge(s_qts, 2 * a + i + 1)
                nc.gpsimd.tensor_tensor(qs[i][:], qT[i][:], ksum[i][:].unsqueeze(2).broadcast_to([128, HALF_I, SEQ]),
                                        ALU.mult).then_inc(s_qs, 1)

            def group(a, more):
                full(a, 0), query_sums(a, 0)
                full(a, 1), query_sums(a, 1)
                for u in POOL_UNITS if more else ():
                    low_unit(a + 2, u)

            low_unit(0, 5), low_unit(1, 3)
            pool.wait_ge(s_cv, 6)
            with pool.Fori(0, GROUPS - 2) as a:
                group(a, True)
            group(GROUPS - 2, False)
            group(GROUPS - 1, False)

            def gather(e, i):
                pool.wait_ge(s_idx, [hi > e for _, hi in LISTS].index(True) + 1)
                if e >= 2:
                    pool.wait_ge(s_xe, 2 * e - 2)
                for r in range(RT):
                    nc.gpsimd.indirect_dma_start(
                        out=got[i][:, r, :], out_offset=None, in_=rows_dram,
                        in_offset=bass.IndirectOffsetOnAxis(ap=idx[:, e, r:r + 1], axis=0)).then_inc(s_got[i], 16)

            def scatter(e, i):
                pool.wait_ge(s_yv, 2 * e + 2)
                if e > 0:
                    pool.wait_ge(s_add, 16 * RT * e)
                pool.wait_ge(s_ost, 16 * GROUPS)
                for r in range(RT):
                    nc.gpsimd.indirect_dma_start(
                        out=out, out_offset=bass.IndirectOffsetOnAxis(ap=idx[:, e, r:r + 1], axis=0),
                        in_=yv[i][:, r, :], in_offset=None, compute_op=ALU.add).then_inc(s_add, 16)

            pool.wait_ge(s_prob, 16)
            pool.wait_ge(s_ost, 16 * GROUPS)
            AHEAD = 4
            for e in range(AHEAD):
                gather(e, e % 2)
            for e in range(EXPERTS):
                scatter(e, e % 2)
                if e + AHEAD < EXPERTS:
                    gather(e + AHEAD, e % 2)
            pool.wait_ge(s_add, 16 * RT * EXPERTS)


def kernel(x, L0_tok_W, L0_tok_b, L0_tok_class_token, L0_tok_pos_embed, L0_attn_qkv_weight, L0_attn_proj_weight,
           L0_attn_proj_bias, L0_ffn_Wr, L0_ffn_W1, L0_ffn_b1, L0_ffn_W2, L0_ffn_b2):
    import concourse.bacc as bacc
    from concourse.bass_utils import run_bass_kernel_spmd

    def cols(a):
        return np.ascontiguousarray(np.asarray(a).reshape(-1, 1))

    xp = np.asarray(x).reshape(GROUPS, GROUP, CHANNELS, GRID, PATCH, GRID, PATCH).transpose(0, 2, 4, 6, 1, 3, 5)
    xp = xp.reshape(GROUPS, IN_D, GP)
    wt = np.asarray(L0_tok_W).T
    arrays = {
        "xmain": xp[:, :IN_D - TAIL].reshape(GROUPS, CHUNKS - 1, 128, GP).transpose(0, 2, 1, 3),
        "xtail": xp[:, IN_D - TAIL:],
        "wmain": wt[:IN_D - TAIL].reshape(CHUNKS - 1, 128, HID).transpose(1, 0, 2),
        "wtail": wt[IN_D - TAIL:],
        "cst": constants(),
        "tokb": cols(L0_tok_b),
        "cls": cols(L0_tok_class_token),
        "posT": np.asarray(L0_tok_pos_embed).T,
        "wqkvT": np.asarray(L0_attn_qkv_weight).T,
        "projT": np.asarray(L0_attn_proj_weight).T,
        "projb": cols(L0_attn_proj_bias),
        "wr": np.asarray(L0_ffn_Wr),
        "w1": np.asarray(L0_ffn_W1),
        "b1": np.asarray(L0_ffn_b1).reshape(EXPERTS, FT, 128).transpose(0, 2, 1),
        "w2": np.asarray(L0_ffn_W2).reshape(EXPERTS, FT, 128, HID).transpose(0, 2, 1, 3),
        "b2": np.asarray(L0_ffn_b2),
    }
    arrays = {n: np.ascontiguousarray(a) for n, a in arrays.items()}
    nc = bacc.Bacc("TRN2", target_bir_lowering=False, num_devices=1)
    aps = {n: nc.dram_tensor(n, a.shape, F32, kind="ExternalInput").ap() for n, a in arrays.items()}
    aps["out"] = nc.dram_tensor("out", (TOKENS, HID), F32, kind="ExternalOutput").ap()
    tower(nc, **aps)
    r = run_bass_kernel_spmd(nc, [arrays], core_ids=[0])
    return np.asarray(r.results[0]["out"]).reshape(IMAGES, SEQ, HID)
```
